# Optimizing a Trainium2 kernel written in Bass

```python
import numpy as np
import jax
import jax.numpy as jnp

def _softmax(x, axis=-1):
    return jax.nn.softmax(x, axis=axis)

def _gelu(x):
    return jax.nn.gelu(x, approximate=True)

def _silu(x):
    return jax.nn.silu(x)

def _sigmoid(x):
    return jax.nn.sigmoid(x)

def _layernorm(x, axis=-1, eps=1e-05):
    m = jnp.mean(x, axis=axis, keepdims=True)
    v = jnp.var(x, axis=axis, keepdims=True)
    return (x - m) / jnp.sqrt(v + eps)

def _scatter_add(tgt, idx, src, axis=0):
    return tgt.at[idx].add(src)

def _segment_sum(src, seg, n):
    return jax.ops.segment_sum(src, seg, n)
kernel_name = 'mk_early_fusion_embed_d1_tok_img768_r4_b027a6'

def setup_inputs(seed: int=0):
    np.random.seed(seed)
    _w = jnp.asarray

    def _rec_inputs():
        import jax
        import jax.numpy as jnp
        _rk = jax.random.key(seed)
        x = -0.000222058 + 0.999998 * jax.random.normal(jax.random.fold_in(_rk, 1), (32, 3, 84, 84), jnp.float32)
        x_txt = jax.random.randint(jax.random.fold_in(_rk, 51), (32, 128), 0, 12564, jnp.int32)
        return (x, x_txt)
    x, x_txt = _rec_inputs()

    def _L0_tok_setup():
        import jax, jax.numpy as jnp
        import numpy as np
        from jax import lax
        HIDDEN = 192
        C_IN = 3
        PATCH = 16
        SIDE = 32
        NUM_PATCHES = SIDE * SIDE

        def _position_ids(nb_h, nb_w):
            boundaries = np.arange(1.0 / SIDE, 1.0, 1.0 / SIDE, dtype=np.float32)
            frac_h = np.arange(0.0, 1.0 - 1e-06, 1.0 / nb_h, dtype=np.float32)
            frac_w = np.arange(0.0, 1.0 - 1e-06, 1.0 / nb_w, dtype=np.float32)
            bh = np.searchsorted(boundaries, frac_h, side='right')
            bw = np.searchsorted(boundaries, frac_w, side='right')
            return jnp.asarray((bh[:, None] * SIDE + bw).reshape(-1), dtype=jnp.int32)
        key = jax.random.key(seed)
        k1, k2, k3 = jax.random.split(key, 3)
        pixel_values = jax.random.normal(k1, (32, C_IN, 128, 128), dtype=jnp.float32)
        conv_w = jax.random.normal(k2, (HIDDEN, C_IN, PATCH, PATCH), dtype=jnp.float32) * 0.02
        conv_b = jnp.zeros((HIDDEN,), dtype=jnp.float32)
        pos_table = jax.random.normal(k3, (NUM_PATCHES, HIDDEN), dtype=jnp.float32) * 0.02
        return {'pixel_values': pixel_values, 'conv_w': conv_w, 'conv_b': conv_b, 'pos_table': pos_table}
    _L0_tok_all = _L0_tok_setup()
    _L0_tok_in = {k: v for k, v in _L0_tok_all.items() if k in ('conv_w', 'conv_b', 'pos_table')}
    del _L0_tok_all

    def _L0_txt_setup():
        import jax, jax.numpy as jnp
        import numpy as np
        VOCAB = 50257
        DIM = 192
        WEIGHT_BIT = 8
        FRACTION_BIT = 10
        key = jax.random.key(seed)
        k1, k2 = jax.random.split(key)
        x = jax.random.randint(k1, (8, 512), 0, VOCAB, dtype=jnp.int64 if jax.config.jax_enable_x64 else jnp.int32)
        weight = jax.random.normal(k2, (VOCAB, DIM), dtype=jnp.float32)
        return {'x': x, 'weight': weight}
    _L0_txt_all = _L0_txt_setup()
    _L0_txt_in = {k: v for k, v in _L0_txt_all.items() if k in ('weight',)}
    del _L0_txt_all

    def _L0_attn_setup():
        import jax, jax.numpy as jnp
        import numpy as np
        HIDDEN = 192
        HEADS = 12
        HEAD_DIM = HIDDEN // HEADS
        ORDER = 5

        def _chebyshev_bias(alphas, seq_len, dtype):
            pos = jnp.arange(seq_len, dtype=dtype)
            denom = dtype.type(max(seq_len - 1, 1)) if hasattr(dtype, 'type') else float(max(seq_len - 1, 1))
            x = jnp.clip((pos[None, :] - pos[:, None]) / float(max(seq_len - 1, 1)), -1.0, 1.0)
            t0 = jnp.ones_like(x)
            polys = [t0, x]
            for _ in range(2, ORDER + 1):
                polys.append(2.0 * x * polys[-1] - polys[-2])
            tk = jnp.stack(polys, axis=-1)
            return jnp.einsum('hk,ijk->hij', alphas, tk)
        key = jax.random.key(seed)
        ks = jax.random.split(key, 8)
        s = 0.02
        return {'hidden_states': jax.random.normal(ks[0], (4, 512, HIDDEN), jnp.float32), 'Wq': jax.random.normal(ks[1], (HIDDEN, HIDDEN), jnp.float32) * s, 'bq': jnp.zeros((HIDDEN,), jnp.float32), 'Wk': jax.random.normal(ks[2], (HIDDEN, HIDDEN), jnp.float32) * s, 'bk': jnp.zeros((HIDDEN,), jnp.float32), 'Wv': jax.random.normal(ks[3], (HIDDEN, HIDDEN), jnp.float32) * s, 'bv': jnp.zeros((HIDDEN,), jnp.float32), 'alphas': jax.random.normal(ks[4], (HEADS, ORDER + 1), jnp.float32) * s}
    _L0_attn_all = _L0_attn_setup()
    _L0_attn_in = {k: v for k, v in _L0_attn_all.items() if k in ('Wq', 'bq', 'Wk', 'bk', 'Wv', 'bv', 'alphas')}
    del _L0_attn_all

    def _L0_ffn_setup():
        import jax, jax.numpy as jnp
        import numpy as np
        B, S, H, I = (4, 512, 192, 384)
        E, K = (3, 2)
        INIT = 0.02

        def _expert(x, gw, uw, dw):
            return jax.nn.silu(x @ gw) * (x @ uw) @ dw
        key = jax.random.key(seed)
        ks = jax.random.split(key, 8)
        f32 = jnp.float32
        return {'x': jax.random.normal(ks[0], (B, S, H), f32), 'shared_gate': jax.random.normal(ks[1], (H, I), f32) * INIT, 'shared_up': jax.random.normal(ks[2], (H, I), f32) * INIT, 'shared_down': jax.random.normal(ks[3], (I, H), f32) * INIT, 'routed_gate': jax.random.normal(ks[4], (E, H, I), f32) * INIT, 'routed_up': jax.random.normal(ks[5], (E, H, I), f32) * INIT, 'routed_down': jax.random.normal(ks[6], (E, I, H), f32) * INIT, 'router_w': jax.random.normal(ks[7], (H, E), f32) * INIT, 'routing_bias': jnp.zeros((E,), f32)}
    _L0_ffn_all = _L0_ffn_setup()
    _L0_ffn_in = {k: v for k, v in _L0_ffn_all.items() if k in ('shared_gate', 'shared_up', 'shared_down', 'routed_gate', 'routed_up', 'routed_down', 'router_w', 'routing_bias')}
    del _L0_ffn_all
    return {'x': x, 'x_txt': x_txt, 'L0_tok_conv_w': _L0_tok_in['conv_w'], 'L0_tok_conv_b': _L0_tok_in['conv_b'], 'L0_tok_pos_table': _L0_tok_in['pos_table'], 'L0_txt_weight': _L0_txt_in['weight'], 'L0_attn_Wq': _L0_attn_in['Wq'], 'L0_attn_bq': _L0_attn_in['bq'], 'L0_attn_Wk': _L0_attn_in['Wk'], 'L0_attn_bk': _L0_attn_in['bk'], 'L0_attn_Wv': _L0_attn_in['Wv'], 'L0_attn_bv': _L0_attn_in['bv'], 'L0_attn_alphas': _L0_attn_in['alphas'], 'L0_ffn_shared_gate': _L0_ffn_in['shared_gate'], 'L0_ffn_shared_up': _L0_ffn_in['shared_up'], 'L0_ffn_shared_down': _L0_ffn_in['shared_down'], 'L0_ffn_routed_gate': _L0_ffn_in['routed_gate'], 'L0_ffn_routed_up': _L0_ffn_in['routed_up'], 'L0_ffn_routed_down': _L0_ffn_in['routed_down'], 'L0_ffn_router_w': _L0_ffn_in['router_w'], 'L0_ffn_routing_bias': _L0_ffn_in['routing_bias']}

def reference(x, x_txt, L0_tok_conv_w, L0_tok_conv_b, L0_tok_pos_table, L0_txt_weight, L0_attn_Wq, L0_attn_bq, L0_attn_Wk, L0_attn_bk, L0_attn_Wv, L0_attn_bv, L0_attn_alphas, L0_ffn_shared_gate, L0_ffn_shared_up, L0_ffn_shared_down, L0_ffn_routed_gate, L0_ffn_routed_up, L0_ffn_routed_down, L0_ffn_router_w, L0_ffn_routing_bias):
    import jax
    import jax.numpy as jnp

    def _L0_tok_ref(pixel_values, conv_w, conv_b, pos_table):
        import jax, jax.numpy as jnp
        import numpy as np
        from jax import lax
        HIDDEN = 192
        C_IN = 3
        PATCH = 16
        SIDE = 32
        NUM_PATCHES = SIDE * SIDE

        def _position_ids(nb_h, nb_w):
            boundaries = np.arange(1.0 / SIDE, 1.0, 1.0 / SIDE, dtype=np.float32)
            frac_h = np.arange(0.0, 1.0 - 1e-06, 1.0 / nb_h, dtype=np.float32)
            frac_w = np.arange(0.0, 1.0 - 1e-06, 1.0 / nb_w, dtype=np.float32)
            bh = np.searchsorted(boundaries, frac_h, side='right')
            bw = np.searchsorted(boundaries, frac_w, side='right')
            return jnp.asarray((bh[:, None] * SIDE + bw).reshape(-1), dtype=jnp.int32)
        B, _, H, W = pixel_values.shape
        nb_h, nb_w = (H // PATCH, W // PATCH)
        patches = lax.conv_general_dilated(pixel_values, conv_w, window_strides=(PATCH, PATCH), padding='VALID', dimension_numbers=('NCHW', 'OIHW', 'NCHW'))
        patches = patches + conv_b[None, :, None, None]
        embeddings = patches.reshape(B, HIDDEN, nb_h * nb_w).transpose(0, 2, 1)
        pos_ids = _position_ids(nb_h, nb_w)
        pos_emb = pos_table[pos_ids]
        return embeddings + pos_emb[None, :, :]

    def _L0_txt_ref(x, weight):
        import jax, jax.numpy as jnp
        import numpy as np
        VOCAB = 50257
        DIM = 192
        WEIGHT_BIT = 8
        FRACTION_BIT = 10
        scale = jnp.asarray(1.0 / 2 ** FRACTION_BIT, dtype=weight.dtype)
        n = 2 ** (WEIGHT_BIT - 1) - 1
        weight_integer = jnp.clip(jnp.round(weight / scale), -n, n - 1)
        emb_int = weight_integer[x]
        return emb_int * scale

    def _L0_attn_ref(hidden_states, Wq, bq, Wk, bk, Wv, bv, alphas):
        import jax, jax.numpy as jnp
        import numpy as np
        HIDDEN = 192
        HEADS = 12
        HEAD_DIM = HIDDEN // HEADS
        ORDER = 5

        def _chebyshev_bias(alphas, seq_len, dtype):
            pos = jnp.arange(seq_len, dtype=dtype)
            denom = dtype.type(max(seq_len - 1, 1)) if hasattr(dtype, 'type') else float(max(seq_len - 1, 1))
            x = jnp.clip((pos[None, :] - pos[:, None]) / float(max(seq_len - 1, 1)), -1.0, 1.0)
            t0 = jnp.ones_like(x)
            polys = [t0, x]
            for _ in range(2, ORDER + 1):
                polys.append(2.0 * x * polys[-1] - polys[-2])
            tk = jnp.stack(polys, axis=-1)
            return jnp.einsum('hk,ijk->hij', alphas, tk)
        b, s, _ = hidden_states.shape

        def split_heads(t):
            return t.reshape(b, s, HEADS, HEAD_DIM).transpose(0, 2, 1, 3)
        q = split_heads(hidden_states @ Wq.T + bq)
        k = split_heads(hidden_states @ Wk.T + bk)
        v = split_heads(hidden_states @ Wv.T + bv)
        scores = jnp.einsum('bhid,bhjd->bhij', q, k) / jnp.sqrt(jnp.asarray(HEAD_DIM, hidden_states.dtype))
        scores = scores + _chebyshev_bias(alphas, s, hidden_states.dtype)[None]
        probs = jax.nn.softmax(scores, axis=-1)
        ctx = jnp.einsum('bhij,bhjd->bhid', probs, v)
        return ctx.transpose(0, 2, 1, 3).reshape(b, s, HIDDEN)

    def _L0_ffn_ref(x, shared_gate, shared_up, shared_down, routed_gate, routed_up, routed_down, router_w, routing_bias):
        import jax, jax.numpy as jnp
        import numpy as np
        B, S, H, I = (4, 512, 192, 384)
        E, K = (3, 2)
        INIT = 0.02

        def _expert(x, gw, uw, dw):
            return jax.nn.silu(x @ gw) * (x @ uw) @ dw
        shared_out = _expert(x, shared_gate, shared_up, shared_down)
        routing_probs = jax.nn.sigmoid(x @ router_w + routing_bias)
        scores, indices = jax.lax.top_k(routing_probs, K)
        scores = scores / scores.sum(axis=-1, keepdims=True)
        combine_w = (jax.nn.one_hot(indices, E, dtype=x.dtype) * scores[..., None]).sum(axis=-2)
        g = jnp.einsum('bsh,ehi->ebsi', x, routed_gate)
        u = jnp.einsum('bsh,ehi->ebsi', x, routed_up)
        h = jax.nn.silu(g) * u
        out_e = jnp.einsum('ebsi,eih->ebsh', h, routed_down)
        combined = jnp.einsum('ebsh,bse->bsh', out_e, combine_w)
        return shared_out + combined
    h = _L0_tok_ref(x, L0_tok_conv_w, L0_tok_conv_b, L0_tok_pos_table)
    h = jnp.concatenate([h, _L0_txt_ref(x_txt, L0_txt_weight)], axis=1)
    h = h + _L0_attn_ref(_layernorm(h, axis=-1), L0_attn_Wq, L0_attn_bq, L0_attn_Wk, L0_attn_bk, L0_attn_Wv, L0_attn_bv, L0_attn_alphas)
    h = h + _L0_ffn_ref(_layernorm(h, axis=-1), L0_ffn_shared_gate, L0_ffn_shared_up, L0_ffn_shared_down, L0_ffn_routed_gate, L0_ffn_routed_up, L0_ffn_routed_down, L0_ffn_router_w, L0_ffn_routing_bias)
    return h

_drawn_inputs = setup_inputs


def setup_inputs(seed=0):
    import zlib

    import numpy as np

    out = dict(_drawn_inputs(seed))
    spreads = {'L0_tok_conv_b': (0.0, 0.1),
     'L0_attn_bq': (0.0, 0.8),
     'L0_attn_bk': (0.0, 2.0),
     'L0_attn_bv': (0.0, 0.1),
     'L0_ffn_routing_bias': (0.0, 2.0)}
    factors = {'L0_attn_Wq': 6.367, 'L0_attn_Wk': 6.078, 'L0_attn_alphas': 8.0, 'L0_ffn_router_w': 40.676}
    for name, (base, spread) in spreads.items():
        noise = np.random.default_rng([zlib.crc32(name.encode()), seed]).standard_normal(out[name].shape)
        drawn = base * np.exp(spread * noise) if base else spread * noise
        out[name] = jnp.asarray(drawn.astype(out[name].dtype))
    for name, factor in factors.items():
        out[name] = (out[name] * factor).astype(out[name].dtype)
    return out
```

```python
from contextlib import ExitStack

import concourse.bass as bass
from concourse import mybir

ALU = mybir.AluOpType
ACT = mybir.ActivationFunctionType
F32 = mybir.dt.float32
F32R = mybir.dt.float32r
BF16 = mybir.dt.bfloat16
I32 = mybir.dt.int32
AX = mybir.AxisListType.X

P = 128
B = 32
NB = 4
G = B // NB
TXT = 128
IMG = 25
S = TXT + IMG
PAD = 160
COLS = NB * PAD
T = NB + 1
D = 192
HEADS = 12
HD = D // HEADS
QUADS = HEADS // 4
KCONV = 6
E = 4
CH = 3
EC = E * CH
HALF = COLS // 2
NORD = 6
LEVELS = 1024.0
QMIN, QMAX = -127.0, 126.0
ROUND = 12582912.0
EPS = 1e-5

C_QK, C_V, C_R, C_GU = 0, 2 * D, 3 * D, 3 * D + 4
WCOLS = 3664
WPIECE = WCOLS // 8
PROD_Q = [0, 1, 0, 1, 0, 2]
PROD_K = [0, 0, 1, 1, 2, 0]
BIAS0 = 6 * HD
MAX0 = 126
BIAS_Q2 = [0, 1, 0]


class Count:

    def __init__(self, handle, per):
        self.handle, self.per = handle, per

    def wait(self, eng, g, k=None):
        eng.wait_ge(self.handle, g * self.per + (self.per if k is None else k))


def build(nc, a):
    ctx = ExitStack()
    with ctx:
        def sb(name, shape, dt=F32):
            return ctx.enter_context(nc.sbuf_tensor(name, shape, dt))

        def sem(name):
            return ctx.enter_context(nc.semaphore(name))

        def count(name, per):
            return Count(sem(name), per)

        ps = ctx.enter_context(nc.psum_tensor("ps", [P, 8, 512], F32))
        w_hi = sb("w_hi", [P, 2, WCOLS], F32R)
        w_lo = sb("w_lo", [P, 2, WCOLS], F32R)
        w_down = sb("w_down", [P, EC, D])
        w_conv = sb("w_conv", [P, KCONV, D])
        ident = sb("ident", [P, P])
        pos_bias = sb("pos_bias", [P, D])
        pos_in = sb("pos_in", [P, D])
        v_bias = sb("v_bias", [P, D])
        qk_bias = sb("qk_bias", [96, 4])
        r_bias = sb("r_bias", [P, T, 3])
        token_ids = sb("token_ids", [P, NB], I32)
        emb = sb("emb", [P, NB, D])
        patches = sb("patches", [P, KCONV, P])
        h1 = sb("h1", [P, T, D])
        h2 = sb("h2", [P, T, D])
        xn = sb("xn", [P, T, 2 * P])
        ctx_n = sb("ctx_n", [P, 2, D])
        stats = sb("stats", [P, T, 6])
        mv = sb("mv", [P, T, 2])
        rstd = sb("rstd", [P, T])
        minus_half = sb("minus_half", [P, T])
        x1t = sb("x1t", [P, 3, COLS], F32R)
        x2t = sb("x2t", [P, 3, COLS], F32R)
        qk_parts = sb("qk_parts", [96, 4, 3, COLS], BF16)
        q_stack = sb("q_stack", [P, HEADS, COLS], BF16)
        k_stack = sb("k_stack", [P, HEADS, COLS], BF16)
        v_txt = sb("v_txt", [P, NB, HEADS, 32])
        v_img = sb("v_img", [P, NB, HEADS, 32])
        spread = sb("spread", [P, NB, P])
        mx = sb("mx", [P, P])
        NM = NB * HEADS + NB * QUADS
        neg_max = sb("neg_max", [NM, 2, P], BF16)
        hid = sb("hid", [P, EC, COLS])
        flat = hid[:].rearrange("p e c -> p (e c)")
        prob_t = [flat[:, i * 4 * S:(i + 1) * 4 * S].rearrange("p (h c) -> p h c", h=4) for i in range(2)]
        prob_i = [flat[:, (8 + i) * S:(9 + i) * S] for i in range(2)]
        qk_rest = flat[0:96, 4600:4600 + 2 * NB * TXT].rearrange("p (k b c) -> p k b c", k=2, b=NB)
        v_all = flat[:, 4000:4000 + D]
        CT0 = 10 * S + 2
        ctxt = flat[:, CT0:CT0 + NB * QUADS * P].rearrange("p (b t c) -> p b t c", b=NB, t=QUADS)
        w_stage = [flat[:, i * 2 * WPIECE:(i + 1) * 2 * WPIECE].rearrange("p (k c) -> p k c", k=2) for i in range(4)]
        ctxi = sb("ctxi", [P, QUADS, P])
        rsum = sb("rsum", [P, 2, HEADS])
        th = sb("th", [P, 2, HALF])
        hg = sb("hg", [P, 2, HALF])
        rt = sb("rt", [P, 8, T, 3])
        rs = sb("rs", [P, 2, T])
        alpha_t = sb("alpha_t", [NORD, HEADS])
        cheb = flat[0:NORD, 4600:4600 + NORD * S]
        q_tab = flat[0:HEADS, 5600:5600 + 3 * NORD * S // 2].bitcast(BF16).rearrange("h (i c) -> h i c", i=3)
        q_tab_rest = flat[0:HEADS, 0:NORD * S]

        w_loaded = [sem(f"w_loaded{i}") for i in range(4)]
        w_high, w_split = sem("w_high"), sem("w_split")
        small_loaded, consts_ready, tab_ready, tab_stored = sem("small_loaded"), sem("consts_ready"), sem("tab_ready"), sem("tab_stored")
        tab_mm, tab_part, tables_in, k_tail_in, pos_ready = sem("tab_mm"), sem("tab_part"), sem("tables_in"), sem("k_tail_in"), sem("pos_ready")
        ids_in, patches_in, emb_in = count("ids_in", 16), count("patches_in", 16), count("emb_in", 16 * NB)
        conv_done = count("conv_done", 1)
        quant = count("quant", 2)
        q_a, q_b, clear_done, passed = count("q_a", 1), count("q_b", 1), sem("clear_done"), sem("passed")
        ln_stat, ln_mv, rstd_ready = count("ln_stat", 2 * T), count("ln_mv", 2 * T), count("rstd_ready", 2)
        var_eps = count("var_eps", 2)
        xn1_done, x1t_done, x1_high, x1_split = count("xn1_done", T), count("x1t_done", T), count("x1_high", T), count("x1_split", T)
        xn2_done, x2t_done, x2_high, x2_split = count("xn2_done", T), count("x2t_done", T), count("x2_high", T), count("x2_split", T)
        qk_done, qk_high, qk_sub, qk_mid, qk_low = (count(n, 8) for n in ("qk_done", "qk_high", "qk_sub", "qk_mid", "qk_low"))
        nm_stored = count("nm_stored", 16 * 3)
        parts_stored, stacks_in = count("parts_stored", 64), count("stacks_in", 16 * 12)
        v_mm, v_done = count("v_mm", 2 * NB + 1), count("v_done", 2 * NB + 1)
        s1_done, max_done = count("s1_done", NB * QUADS), count("max_done", NB * QUADS)
        mt_done, nm_high, nm_done, nm_in = count("mt_done", 1), count("nm_high", 1), count("nm_done", 1), count("nm_in", 16 * NB)
        s2_done, exp_done, pv_done, pv_copied = (count(n, NB * QUADS) for n in ("s2_done", "exp_done", "pv_done", "pv_copied"))
        ct_done, ct_recip, ct_norm, h2_done = count("ct_done", T), count("ct_recip", T), count("ct_norm", T), count("h2_done", T)
        r_mm, r_z, r_exp, r_step, gates_ready = count("r_mm", 1), count("r_z", 1), count("r_exp", 1), count("r_step", 8), count("gates_ready", 1)
        gu_done, tanh_done, hg_done, hid_done = count("gu_done", 4 * EC), count("tanh_done", 2 * EC), count("hg_done", 2 * EC), count("hid_done", 2 * EC)
        down_done, comb_half, comb_done, out_stored = count("down_done", 2 * T), count("comb_half", 2 * T), count("comb_done", 2 * T), count("out_stored", 16 * (1 + NB))

        parts_d = nc.dram_tensor("parts_scratch", (2, 3, D, COLS), BF16).ap()
        nm_d = nc.dram_tensor("neg_max_scratch", (2, NB, HEADS, S), BF16).ap()
        qtab_d = nc.dram_tensor("qtab_scratch", (3, NORD, HEADS, S), BF16).ap()

        QK_BANK = [3, 4, 6, 7]
        GU_BANKS = [(0, 1), (2, 5), (6, 7)]

        out_g = a["out"].rearrange("(g b) s d -> g b s d", b=NB)

        def qk_source(i):
            if i % 2 == 0:
                return ps[0:96, QK_BANK[i % 4], 0:NB * TXT].rearrange("p (b c) -> p b c", b=NB)
            return ps[0:96, QK_BANK[i % 4], 0:NB * 32].rearrange("p (b c) -> p b c", b=NB)[:, :, 0:IMG]

        def qk_part(i, k):
            c = slice(0, TXT) if i % 2 == 0 else slice(TXT, S)
            return qk_parts[:, i // 2, k].rearrange("p (b c) -> p b c", b=NB)[:, :, c]

        def qk_rest_of(i):
            return qk_rest[:, i % 2, :, 0:TXT if i % 2 == 0 else IMG]

        def pass_waits(eng):
            eng.sem_inc(passed, 1)

        block = ctx.enter_context(nc.Block())

        @block.sync
        def _(sp):
            def load_tokens(n):
                if not isinstance(n, int) or n > 0:
                    emb_in.wait(sp, n - 1)
                    pass_waits(sp)
                    conv_done.wait(sp, n - 1)
                    pass_waits(sp)
                sp.dma_start(token_ids[:], a["ids"][n]).then_inc(ids_in.handle, 16)
                sp.dma_start(patches[:], a["patches"][n]).then_inc(patches_in.handle, 16)

            def store_parts(n):
                stacks_in.wait(sp, n, 0)
                for t in range(4):
                    qk_low.wait(sp, n, 2 * t + 2)
                    qk_mid.wait(sp, n, 2 * t + 2)
                    r0 = 96 * (t % 2)
                    sp.dma_start(parts_d[t // 2, :, r0:r0 + 96, :].rearrange("s r c -> r s c"),
                                 qk_parts[:, t]).then_inc(parts_stored.handle, 16)

            def load_stacks(n):
                parts_stored.wait(sp, n)
                pass_waits(sp)
                s2_done.wait(sp, n, 0)
                for i in range(6):
                    for qk, stack, parts in ((0, q_stack, PROD_Q), (1, k_stack, PROD_K)):
                        sp.dma_start(stack[HD * i:HD * (i + 1)],
                                     parts_d[qk, parts[i]].rearrange("(h d) c -> d h c", d=HD)
                                     ).then_inc(stacks_in.handle, 16)

            def load_neg_max(n):
                nm_high.wait(sp, n)
                nm_done.wait(sp, n)
                nb = NB * HEADS
                sp.dma_start(nm_d[:, :, :, 0:TXT].rearrange("i b h c -> (b h) i c"), neg_max[0:nb]
                             ).then_inc(nm_stored.handle, 16)
                for i in range(2):
                    sp.dma_start(nm_d[i, :, :, TXT:S].rearrange("b (t q) c -> (b t) q c", q=4),
                                 neg_max[nb:NM, i].rearrange("t (q s) -> t q s", q=4)[:, :, 0:IMG]
                                 ).then_inc(nm_stored.handle, 16)
                nm_stored.wait(sp, n)
                for b in range(NB):
                    sp.dma_start(q_stack[MAX0:P, :, PAD * b:PAD * b + S], nm_d[:, b]).then_inc(nm_in.handle, 16)

            def store_out(n):
                comb_done.wait(sp, n)
                pass_waits(sp)
                sp.dma_start(out_g[n, :, IMG:S, :].rearrange("b s d -> s b d"), h2[:, 0:NB, :]
                             ).then_inc(out_stored.handle, 16)
                for b in range(NB):
                    sp.dma_start(out_g[n, b, 0:IMG, :], h2[32 * b:32 * b + IMG, NB, :]
                                 ).then_inc(out_stored.handle, 16)

            load_tokens(0)
            for i in range(8):
                if i >= 4:
                    sp.wait_ge(w_split, i - 3)
                sp.dma_start(w_stage[i % 4], a["w_split"][i]).then_inc(w_loaded[i % 4], 16)
                if i == 3:
                    sp.dma_start(w_down[:], a["w_down"]).then_inc(small_loaded, 16)
                if i == 0:
                    sp.dma_start(w_conv[:], a["w_conv"]).then_inc(small_loaded, 16)
                    sp.dma_start(ident[:], a["ident"]).then_inc(small_loaded, 16)
                    sp.dma_start(pos_in[:], a["pos"]).then_inc(small_loaded, 16)
                    sp.dma_start(pos_bias[:], a["conv_b"]).then_inc(small_loaded, 16)
                    sp.dma_start(v_bias[:], a["bv"]).then_inc(small_loaded, 16)
                    sp.dma_start(qk_bias[:], a["bqk"]).then_inc(small_loaded, 16)
                    sp.dma_start(r_bias[:], a["r_bias"]).then_inc(small_loaded, 16)
                    sp.dma_start(alpha_t[:], a["alpha_t"]).then_inc(small_loaded, 16)
                    sp.dma_start(cheb, a["cheb"]).then_inc(small_loaded, 16)
                    sp.dma_start(spread[:], a["spread"]).then_inc(small_loaded, 16)
            sp.wait_ge(consts_ready, 2)
            sp.dma_start(k_stack[BIAS0:P].rearrange("r h c -> r (h c)"), a["k_tail"]).then_inc(k_tail_in, 16)
            sp.wait_ge(tab_ready, 1)
            for i in range(3):
                sp.dma_start(qtab_d[i].rearrange("n h s -> h n s"),
                             q_tab[:, i, :].rearrange("h (n s) -> h n s", n=NORD)).then_inc(tab_stored, 16)
            sp.wait_ge(tab_stored, 48)
            for b in range(NB):
                c0 = PAD * b
                for i in range(3):
                    sp.dma_start(q_stack[BIAS0 + NORD * i:BIAS0 + NORD * (i + 1), :, c0:c0 + S], qtab_d[i]
                                 ).then_inc(tables_in, 16)
                    r = BIAS0 + 3 * NORD + (NORD - 2) * i
                    sp.dma_start(q_stack[r:r + NORD - 2, :, c0:c0 + S], qtab_d[BIAS_Q2[i], 2:NORD]
                                 ).then_inc(tables_in, 16)
            store_parts(0)
            load_stacks(0)

            def group(g, first=False, last=False):
                if not last:
                    load_tokens(g + 1)
                load_neg_max(g)
                if not first:
                    store_out(g - 1)
                if not last:
                    store_parts(g + 1)
                    load_stacks(g + 1)

            group(0, first=True)
            with sp.Fori(1, G - 1) as g:
                group(g)
            group(G - 1, last=True)
            store_out(G - 1)
            out_stored.wait(sp, G - 1)

        @block.gpsimd
        def _(pool):
            nc.gpsimd.memset(minus_half[:], -0.5).then_inc(consts_ready, 1)

            def gather(n):
                ids_in.wait(pool, n)
                quant.wait(pool, n, 0)
                pass_waits(pool)
                for b in range(NB):
                    nc.gpsimd.indirect_dma_start(
                        out=emb[:, b, :], out_offset=None, in_=a["table"],
                        in_offset=bass.IndirectOffsetOnAxis(ap=token_ids[:, b:b + 1], axis=0),
                    ).then_inc(emb_in.handle, 16)

            def inv_std(n, which):
                var_eps.wait(pool, n, which + 1)
                nc.gpsimd.tensor_tensor(rstd[:], rstd[:], minus_half[:], ALU.pow).then_inc(rstd_ready.handle, 1)

            def low_parts(n):
                for i in range(8):
                    qk_mid.wait(pool, n, i + 1)
                    nc.gpsimd.tensor_tensor(qk_part(i, 2), qk_rest_of(i), qk_part(i, 1), ALU.subtract
                                            ).then_inc(qk_low.handle, 1)

            gather(0)
            inv_std(0, 0)
            low_parts(0)

            def group(g, last=False):
                if not last:
                    gather(g + 1)
                inv_std(g, 1)
                if not last:
                    inv_std(g + 1, 0)
                    low_parts(g + 1)

            with pool.Fori(0, G - 1) as g:
                group(g)
            group(G - 1, last=True)

        @block.scalar
        def _(act):
            def high_x(n, done, high, xt, bank):
                for t in range(T):
                    done.wait(act, n, t + 1)
                    nc.scalar.activation(xt[:, 0:2, P * t:P * (t + 1)],
                                         ps[:, bank + t % 2, 0:2 * P].rearrange("p (k c) -> p k c", k=2), ACT.Copy
                                         ).then_inc(high.handle, 1)

            def high_qk(n):
                parts_stored.wait(act, n, 0)
                for i in range(8):
                    qk_done.wait(act, n, i + 1)
                    nc.scalar.activation(qk_part(i, 0), qk_source(i), ACT.Identity, bias=qk_bias[:, i // 2:i // 2 + 1]
                                         ).then_inc(qk_high.handle, 1)

            def exps(g):
                for s in range(NB * QUADS):
                    bank = 3 * (s % 2)
                    s2_done.wait(act, g, s + 1)
                    if s >= 2:
                        pv_done.wait(act, g, s - 1)
                    nc.scalar.activation(prob_t[s % 2].rearrange("p (k h) c -> p k (h c)", k=2),
                                         ps[:, bank:bank + 2, 0:2 * S], ACT.Exp, scale=0.25)
                    nc.scalar.activation(prob_i[s % 2], ps[:, bank + 2, 0:S], ACT.Exp, scale=0.25
                                         ).then_inc(exp_done.handle, 1)

            def router_exp(g):
                r_z.wait(act, g)
                nc.scalar.activation(rt[:, 1], rt[:, 0], ACT.Exp, scale=-1.0).then_inc(r_exp.handle, 1)

            def tanhs(g):
                for j in range(2 * EC):
                    gu_done.wait(act, g, 2 * j + 1)
                    if j >= 2:
                        hg_done.wait(act, g, j - 1)
                    nc.scalar.activation(th[:, j % 2], ps[:, GU_BANKS[j % 3][0], 0:HALF], ACT.Tanh, scale=0.5
                                         ).then_inc(tanh_done.handle, 1)

            def neg_high(g):
                mt_done.wait(act, g)
                nc.scalar.activation(neg_max[:, 0], ps[0:NM, 5, 0:P], ACT.Copy, scale=-1.0
                                     ).then_inc(nm_high.handle, 1)

            for i in range(8):
                act.wait_ge(w_loaded[i % 4], 16 * (i // 4 + 1))
                nc.scalar.activation(w_hi[:, :, WPIECE * i:WPIECE * (i + 1)], w_stage[i % 4], ACT.Copy
                                     ).then_inc(w_high, 1)
            act.wait_ge(small_loaded, 176)
            act.wait_ge(consts_ready, 2)
            high_x(0, x1t_done, x1_high, x1t, 0)
            high_qk(0)

            def group(g, last=False):
                neg_high(g)
                exps(g)
                high_x(g, x2t_done, x2_high, x2t, 3)
                router_exp(g)
                if not last:
                    high_x(g + 1, x1t_done, x1_high, x1t, 0)
                    high_qk(g + 1)
                tanhs(g)

            with act.Fori(0, G - 1) as g:
                group(g)
            group(G - 1, last=True)

        @block.vector
        def _(dve):
            v = nc.vector

            def quantise(n):
                emb_in.wait(dve, n)
                v.tensor_scalar(emb[:], emb[:], LEVELS, QMIN, ALU.mult, ALU.max).then_inc(q_a.handle, 1)
                q_a.wait(dve, n)
                v.tensor_scalar(emb[:], emb[:], QMAX, ROUND, ALU.min, ALU.add).then_inc(q_b.handle, 1)
                q_b.wait(dve, n)
                v.tensor_scalar(h1[:, 0:NB], emb[:], ROUND, 1.0 / LEVELS, ALU.subtract, ALU.mult
                                ).then_inc(quant.handle, 1)
                conv_done.wait(dve, n)
                v.tensor_tensor(h1[:, NB], ps[:, 2, 0:D], pos_bias[:], ALU.add).then_inc(quant.handle, 1)
                quant.wait(dve, n)

            def norm(n, which, src, done):
                k0 = which * T
                for t in range(T):
                    if which:
                        h2_done.wait(dve, n, t + 1)
                    v.bn_stats(stats[:, t], src[:, t]).then_inc(ln_stat.handle, 1)
                for t in range(T):
                    stat_wait(n, which, t + 1)
                    pass_waits(dve)
                    v.bn_aggr(mv[:, t], stats[:, t]).then_inc(ln_mv.handle, 1)
                mv_wait(n, which)
                v.tensor_scalar(rstd[:], mv[:, :, 1], EPS, None, ALU.add).then_inc(var_eps.handle, 1)
                rstd_wait(n, which)
                for t in range(T):
                    m, r = mv[:, t, 0:1], rstd[:, t:t + 1]
                    v.tensor_scalar(xn[:, t, 0:D], src[:, t], m, r, ALU.subtract, ALU.mult)
                    v.tensor_scalar(xn[:, t, D:2 * P], src[:, t, P:D], m, r, ALU.subtract, ALU.mult
                                    ).then_inc(done.handle, 1)

            def split_x(n, high, split, xt, bank):
                for t in range(T):
                    high.wait(dve, n, t + 1)
                    src, c = ps[:, bank + t % 2, 0:2 * P], slice(P * t, P * (t + 1))
                    v.tensor_tensor(xt[:, 2, c], src[:, 0:P], xt[:, 0, c].bitcast(F32), ALU.subtract)
                    v.tensor_tensor(xt[64:P, 1, c], src[64:P, P:2 * P], xt[64:P, 1, c].bitcast(F32), ALU.subtract
                                    ).then_inc(split.handle, 1)

            def split_qk(n):
                for i in range(8):
                    qk_high.wait(dve, n, i + 1)
                    if i >= 2:
                        qk_low.wait(dve, n, i - 1)
                    v.scalar_tensor_tensor(qk_rest_of(i), qk_source(i), qk_bias[:, i // 2:i // 2 + 1], qk_part(i, 0),
                                           ALU.add, ALU.subtract).then_inc(qk_sub.handle, 1)
                    qk_sub.wait(dve, n, i + 1)
                    v.tensor_copy(qk_part(i, 1), qk_rest_of(i)).then_inc(qk_mid.handle, 1)

            def values(g):
                v_mm.wait(dve, g, 1)
                v.tensor_tensor(v_all, ps[:, 7, 0:D], v_bias[:], ALU.add).then_inc(v_done.handle, 1)
                for b in range(NB):
                    v_mm.wait(dve, g, 2 * b + 2)
                    v.tensor_tensor(v_txt[:, b, :, 0:HD], ps[:, 6, 0:D].rearrange("p (h d) -> p h d", d=HD),
                                    v_bias[:].rearrange("p (h d) -> p h d", d=HD), ALU.add
                                    ).then_inc(v_done.handle, 1)
                    v_mm.wait(dve, g, 2 * b + 3)
                    for q in range(4):
                        rows = slice(32 * q, 32 * q + IMG)
                        ins = v.tensor_copy(v_img[rows, b].rearrange("p (t q) d -> p q t d", q=4)[:, q, :, 0:HD],
                                            ps[rows, 7, 0:D].rearrange("p (t q d) -> p q t d", q=4, d=HD)[:, q])
                    ins.then_inc(v_done.handle, 1)

            def maxima(g, s):
                b, t = s // QUADS, s % QUADS
                s1_done.wait(dve, g, s + 1)
                c = HEADS * b + 4 * t
                v.tensor_reduce(mx[:, c:c + 4].rearrange("p (k h) -> p k h", k=2),
                                ps[:, 0:2, 0:2 * S].rearrange("p k (h c) -> p k h c", h=2), AX, ALU.max)
                c = NB * HEADS + QUADS * b + t
                v.tensor_reduce(mx[:, c:c + 1], ps[:, 2, 0:S], AX, ALU.max).then_inc(max_done.handle, 1)

            def neg_low(g):
                nm_high.wait(dve, g)
                v.scalar_tensor_tensor(neg_max[:, 1], ps[0:NM, 5, 0:P], -1.0, neg_max[:, 0],
                                       ALU.mult, ALU.subtract).then_inc(nm_done.handle, 1)

            def copy_ctx(g):
                for s in range(NB * QUADS):
                    b, t = s // QUADS, s % QUADS
                    pv_done.wait(dve, g, s + 1)
                    v.tensor_copy(ctxt[:, b, t], ps[:, 6 + s % 2, 0:TXT])
                    v.tensor_copy(ctxi[:, t, 32 * b:32 * b + IMG], ps[:, 6 + s % 2, TXT:S]
                                  ).then_inc(pv_copied.handle, 1)

            def add_ctx(g):
                out_stored.wait(dve, g, 0)
                for t in range(T):
                    c = ps[:, 6 + t % 2, 0:HEADS * 32].rearrange("p (h d) -> p h d", d=32)
                    ct_done.wait(dve, g, t + 1)
                    v.reciprocal(rsum[:, t % 2], c[:, :, HD]).then_inc(ct_recip.handle, 1)
                    ct_recip.wait(dve, g, t + 1)
                    v.tensor_tensor(ctx_n[:, t % 2].rearrange("p (h d) -> p h d", d=HD), c[:, :, 0:HD],
                                    rsum[:, t % 2].unsqueeze(2).broadcast_to([P, HEADS, HD]), ALU.mult
                                    ).then_inc(ct_norm.handle, 1)
                    ct_norm.wait(dve, g, t + 1)
                    v.tensor_tensor(h2[:, t], ctx_n[:, t % 2], h1[:, t], ALU.add).then_inc(h2_done.handle, 1)

            def gates(g):
                step = [0]

                def then(ins):
                    step[0] += 1
                    ins.then_inc(r_step.handle, 1)
                    r_step.wait(dve, g, step[0])

                z, e, p, keep, w, tmp = rt[:, 0], rt[:, 1], rt[:, 2], rt[:, 3], rt[:, 4], rt[:, 5]
                r_mm.wait(dve, g)
                v.tensor_tensor(z, ps[:, 5, 0:4 * T].rearrange("p (t e) -> p t e", e=4)[:, :, 0:3], r_bias[:], ALU.add
                                ).then_inc(r_z.handle, 1)
                r_exp.wait(dve, g)
                then(v.tensor_scalar(e, e, 1.0, None, ALU.add))
                then(v.reciprocal(p, e))
                v.tensor_tensor(tmp[:, :, 0], p[:, :, 0], p[:, :, 1], ALU.is_ge)
                v.tensor_tensor(tmp[:, :, 1], p[:, :, 0], p[:, :, 2], ALU.is_ge)
                then(v.tensor_tensor(tmp[:, :, 2], p[:, :, 1], p[:, :, 2], ALU.is_ge))
                v.tensor_tensor(keep[:, :, 0], tmp[:, :, 0], tmp[:, :, 1], ALU.max)
                v.tensor_tensor(keep[:, :, 2], tmp[:, :, 1], tmp[:, :, 2], ALU.min)
                then(v.tensor_scalar(rt[:, 6, :, 0], tmp[:, :, 0], -1.0, 1.0, ALU.mult, ALU.add))
                v.tensor_tensor(keep[:, :, 1], rt[:, 6, :, 0], tmp[:, :, 2], ALU.max)
                then(v.tensor_scalar(keep[:, :, 2], keep[:, :, 2], -1.0, 1.0, ALU.mult, ALU.add))
                then(v.tensor_tensor(w, keep, p, ALU.mult))
                then(v.tensor_reduce(rs[:, 0], w, AX, ALU.add))
                then(v.reciprocal(rs[:, 1], rs[:, 0]))
                v.scalar_tensor_tensor(rt[:, 7], w, 0.5, rs[:, 1].unsqueeze(2).broadcast_to([P, T, 3]),
                                       ALU.mult, ALU.mult).then_inc(gates_ready.handle, 1)

            def hidden(g, last):
                if not last:
                    qk_low.wait(dve, g + 1)
                for j in range(2 * EC):
                    hf, ec = j // EC, j % EC
                    bg, bu = GU_BANKS[j % 3]
                    tanh_done.wait(dve, g, j + 1)
                    v.scalar_tensor_tensor(hg[:, j % 2], th[:, j % 2], 1.0, ps[:, bg, 0:HALF], ALU.add, ALU.mult
                                           ).then_inc(hg_done.handle, 1)
                    hg_done.wait(dve, g, j + 1)
                    gu_done.wait(dve, g, 2 * j + 2)
                    v.tensor_tensor(hid[:, ec, HALF * hf:HALF * (hf + 1)], hg[:, j % 2], ps[:, bu, 0:HALF], ALU.mult
                                    ).then_inc(hid_done.handle, 1)

            def combine(n, i):
                t, pr = i // 2, i % 2
                down_done.wait(dve, n, i + 1)
                if pr:
                    comb_done.wait(dve, n, i)
                for k in range(2):
                    gate = 0.5 if (pr, k) == (0, 0) else rt[:, 7, t, 2 * pr + k - 1:2 * pr + k]
                    v.scalar_tensor_tensor(h2[:, t], ps[:, 3 + pr, D * k:D * (k + 1)], gate, h2[:, t],
                                           ALU.mult, ALU.add).then_inc((comb_done if k else comb_half).handle, 1)
                    if not k:
                        comb_half.wait(dve, n, i + 1)

            def stat_wait(n, which, k):
                ln_stat.wait(dve, n, ln_at(which) + k)

            def mv_wait(n, which):
                ln_mv.wait(dve, n, ln_at(which) + T)

            def rstd_wait(n, which):
                rstd_ready.wait(dve, n, 1 + which)

            def ln_at(which):
                return which * T

            v.memset(qk_parts[:], 0.0)
            v.memset(mx[:], 0.0)
            v.memset(q_stack[64:P].rearrange("p h c -> p (h c)"), 0.0)
            v.memset(v_txt[:], 0.0)
            v.memset(v_img[:], 0.0)
            v.memset(ctxi[:], 1.0).then_inc(clear_done, 1)
            dve.wait_ge(clear_done, 1)
            v.memset(v_txt[:, :, :, HD:HD + 1], 1.0)
            for q in range(4):
                rows = slice(32 * q, 32 * q + IMG)
                ins = v.memset(v_img[rows].rearrange("p b (t q) d -> p q (b t) d", q=4)[:, q, :, HD:HD + 1], 1.0)
            ins.then_inc(consts_ready, 1)
            dve.wait_ge(consts_ready, 2)
            dve.wait_ge(small_loaded, 176)
            v.tensor_tensor(pos_bias[:], pos_bias[:], pos_in[:], ALU.add).then_inc(pos_ready, 1)
            for i in range(8):
                dve.wait_ge(w_high, i + 1)
                c = slice(WPIECE * i, WPIECE * (i + 1))
                v.tensor_tensor(w_lo[:, :, c], w_stage[i % 4], w_hi[:, :, c].bitcast(F32), ALU.subtract
                                ).then_inc(w_split, 1)
            dve.wait_ge(tab_mm, 1)
            tab = ps[0:HEADS, 6:8, 0:NORD * S // 2]
            part = [q_tab[:, i].rearrange("h (k c) -> h k c", k=2) for i in range(3)]
            rest = q_tab_rest.rearrange("h (k c) -> h k c", k=2)
            v.tensor_copy(part[0], tab).then_inc(tab_part, 1)
            dve.wait_ge(tab_part, 1)
            dve.wait_ge(w_split, 8)
            v.tensor_tensor(rest, tab, part[0], ALU.subtract).then_inc(tab_part, 1)
            dve.wait_ge(tab_part, 2)
            v.tensor_copy(part[1], rest).then_inc(tab_part, 1)
            dve.wait_ge(tab_part, 3)
            v.tensor_tensor(part[2], rest, part[1], ALU.subtract).then_inc(tab_ready, 1)
            dve.wait_ge(pos_ready, 1)

            quantise(0)
            norm(0, 0, h1, xn1_done)
            split_x(0, x1_high, x1_split, x1t, 0)
            split_qk(0)

            def group(g, first=False, last=False):
                if first:
                    for s in range(NB * QUADS):
                        maxima(g, s)
                else:
                    for s in range(2 * T):
                        maxima(g, s)
                        combine(g - 1, s)
                    for s in range(2 * T, NB * QUADS):
                        maxima(g, s)
                neg_low(g)
                values(g)
                copy_ctx(g)
                add_ctx(g)
                norm(g, 1, h2, xn2_done)
                split_x(g, x2_high, x2_split, x2t, 3)
                gates(g)
                if not last:
                    quantise(g + 1)
                    x2t_done.wait(dve, g)
                    norm(g + 1, 0, h1, xn1_done)
                    split_x(g + 1, x1_high, x1_split, x1t, 0)
                    split_qk(g + 1)
                hidden(g, last)

            group(0, first=True)
            with dve.Fori(1, G - 1) as g:
                group(g)
            group(G - 1, last=True)
            for s in range(2 * T):
                combine(G - 1, s)

        @block.tensor
        def _(pe):
            mm = nc.tensor.matmul

            def split_mm(out, w, x, lhs_is_x):
                passes = ((w_hi, 0, 0), (w_hi, 0, 2), (w_lo, 0, 0), (w_hi, 1, 1), (w_lo, 1, 1))
                for i, (wt, wk, xk) in enumerate(passes):
                    l, r = wt[:, wk, w], x(xk)
                    if lhs_is_x:
                        l, r = r, l
                    ins = mm(out, l, r, start=(i == 0), stop=(i == 4))
                return ins

            def conv(n):
                patches_in.wait(pe, n)
                for c in range(KCONV):
                    ins = mm(ps[:, 2, 0:D], patches[:, c], w_conv[:, c], start=(c == 0), stop=(c == KCONV - 1))
                ins.then_inc(conv_done.handle, 1)

            def turn(n, xn_done, done, split, bank):
                for t in range(T):
                    xn_done.wait(pe, n, t + 1)
                    if t >= 2:
                        split.wait(pe, n, t - 1)
                    bk = bank + t % 2
                    nc.tensor.transpose(ps[:, bk, 0:P], xn[:, t, 0:P], ident[:])
                    nc.tensor.transpose(ps[:, bk, P:2 * P], xn[:, t, P:2 * P], ident[:]
                                        ).then_inc(done.handle, 1)

            def qk(n):
                x1_split.wait(pe, n)
                for i in range(8):
                    c = slice(0, NB * TXT) if i % 2 == 0 else slice(NB * TXT, T * P)
                    at = C_QK + 96 * (i // 2)
                    if i >= 4:
                        qk_sub.wait(pe, n, i - 3)
                    split_mm(ps[0:96, QK_BANK[i % 4], 0:c.stop - c.start], slice(at, at + 96),
                             lambda k: x1t[:, k, c], False).then_inc(qk_done.handle, 1)

            def values(g):
                img = slice(NB * TXT, T * P)
                split_mm(ps[:, 7, 0:D], slice(C_V, C_V + D), lambda k: x1t[:, k, img], True).then_inc(v_mm.handle, 1)
                for b in range(NB):
                    if b:
                        v_done.wait(pe, g, 2 * b)
                    split_mm(ps[:, 6, 0:D], slice(C_V, C_V + D), lambda k: x1t[:, k, P * b:P * (b + 1)], True
                             ).then_inc(v_mm.handle, 1)
                    v_done.wait(pe, g, 2 * b + 1)
                    mm(ps[:, 7, 0:D], spread[:, b], v_all, start=True, stop=True).then_inc(v_mm.handle, 1)

            def scores_by_query(g, s):
                b, t = s // QUADS, s % QUADS
                if s:
                    max_done.wait(pe, g, s)
                c = PAD * b
                for i in range(4):
                    mm(ps[:, i // 2, S * (i % 2):S * (i % 2 + 1)], q_stack[0:MAX0, 4 * t + i, c:c + TXT],
                       k_stack[0:MAX0, 4 * t + i, c:c + S], start=True, stop=True)
                for i in range(4):
                    ins = mm(ps[32 * i:32 * i + 32, 2, 0:S], q_stack[0:MAX0, 4 * t + i, c + TXT:c + PAD],
                             k_stack[0:MAX0, 4 * t + i, c:c + S], start=True, stop=True)
                ins.then_inc(s1_done.handle, 1)

            def scores_by_key(g, s):
                b, t = s // QUADS, s % QUADS
                if s >= 2:
                    exp_done.wait(pe, g, s - 1)
                c, bank = PAD * b, 3 * (s % 2)
                for i in range(4):
                    mm(ps[:, bank + i // 2, S * (i % 2):S * (i % 2 + 1)], k_stack[:, 4 * t + i, c:c + TXT],
                       q_stack[:, 4 * t + i, c:c + S], start=True, stop=True)
                for i in range(4):
                    ins = mm(ps[32 * i:32 * i + 32, bank + 2, 0:S], k_stack[:, 4 * t + i, c + TXT:c + PAD],
                             q_stack[:, 4 * t + i, c:c + S], start=True, stop=True)
                ins.then_inc(s2_done.handle, 1)

            def context(g, s):
                b, t = s // QUADS, s % QUADS
                exp_done.wait(pe, g, s + 1)
                if s >= 2:
                    pv_copied.wait(pe, g, s - 1)
                bank = 6 + s % 2
                mm(ps[:, bank, 0:S], v_img[:, b, 4 * t:4 * t + 4].rearrange("p h d -> p (h d)"), prob_i[s % 2],
                   start=True, stop=False)
                for i in range(4):
                    ins = mm(ps[32 * i:32 * i + 32, bank, 0:S], v_txt[:, b, 4 * t + i], prob_t[s % 2][:, i],
                             start=False, stop=True)
                ins.then_inc(pv_done.handle, 1)

            def turn_ctx(g):
                pv_copied.wait(pe, g)
                for t in range(T):
                    if t >= 2:
                        h2_done.wait(pe, g, t - 1)
                    for k in range(QUADS):
                        src = ctxt[:, t, k] if t < NB else ctxi[:, k]
                        ins = nc.tensor.transpose(ps[:, 6 + t % 2, P * k:P * (k + 1)], src, ident[:])
                    ins.then_inc(ct_done.handle, 1)

            def router(g):
                x2_split.wait(pe, g)
                for t in range(T):
                    ins = split_mm(ps[:, 5, 4 * t:4 * t + 4], slice(C_R, C_R + 4),
                                   lambda k: x2t[:, k, P * t:P * (t + 1)], True)
                ins.then_inc(r_mm.handle, 1)

            def gate_up(g, last):
                r_z.wait(pe, g)
                if not last:
                    qk_sub.wait(pe, g + 1)
                for j in range(2 * EC):
                    hf, ec = j // EC, j % EC
                    if j >= 3:
                        hid_done.wait(pe, g, j - 2)
                    for k in range(2):
                        c = C_GU + 2 * P * ec + P * k
                        split_mm(ps[:, GU_BANKS[j % 3][k], 0:HALF], slice(c, c + P),
                                 lambda x: x2t[:, x, HALF * hf:HALF * (hf + 1)], False).then_inc(gu_done.handle, 1)

            def down(n, i):
                t, pr = i // 2, i % 2
                if i == 0:
                    hid_done.wait(pe, n)
                if i >= 2:
                    comb_done.wait(pe, n, i - 1)
                for k in range(2):
                    for c in range(CH):
                        ec = CH * (2 * pr + k) + c
                        ins = mm(ps[:, 3 + pr, D * k:D * (k + 1)], hid[:, ec, P * t:P * (t + 1)], w_down[:, ec],
                                 start=(c == 0), stop=(c == CH - 1))
                ins.then_inc(down_done.handle, 1)

            pe.wait_ge(small_loaded, 176)
            pe.wait_ge(w_split, 8)
            for i in range(2):
                n = NORD * S // 2
                ins = mm(ps[0:HEADS, 6 + i, 0:n], alpha_t[:], cheb[:, n * i:n * (i + 1)], start=True, stop=True)
            ins.then_inc(tab_mm, 1)
            conv(0)
            turn(0, xn1_done, x1t_done, x1_split, 0)
            pe.wait_ge(tab_ready, 1)
            qk(0)
            pe.wait_ge(tables_in, 16 * 6 * NB)
            pe.wait_ge(k_tail_in, 16)
            pe.wait_ge(consts_ready, 2)

            def group(g, first=False, last=False):
                stacks_in.wait(pe, g)
                if first:
                    for s in range(NB * QUADS):
                        scores_by_query(g, s)
                else:
                    for s in range(2 * T):
                        if s == 0:
                            hid_done.wait(pe, g - 1)
                        scores_by_query(g, s)
                        down(g - 1, s)
                    for s in range(2 * T, NB * QUADS):
                        scores_by_query(g, s)
                max_done.wait(pe, g)
                nc.tensor.transpose(ps[:, 5, 0:P], mx[:], ident[:]).then_inc(mt_done.handle, 1)
                values(g)
                nm_in.wait(pe, g)
                if not first:
                    comb_done.wait(pe, g - 1)
                v_done.wait(pe, g)
                for s in range(NB * QUADS + 1):
                    if s < NB * QUADS:
                        scores_by_key(g, s)
                    if s:
                        context(g, s - 1)
                turn_ctx(g)
                turn(g, xn2_done, x2t_done, x2_split, 3)
                router(g)
                if not last:
                    conv(g + 1)
                    turn(g + 1, xn1_done, x1t_done, x1_split, 0)
                    qk(g + 1)
                gate_up(g, last)

            group(0, first=True)
            with pe.Fori(1, G - 1) as g:
                group(g)
            group(G - 1, last=True)
            for s in range(2 * T):
                down(G - 1, s)


def chebyshev_tables():
    import numpy as np

    def orders(x):
        t = [np.ones_like(x), x]
        while len(t) < NORD:
            t.append(2 * x * t[-1] - t[-2])
        return np.stack(t)

    c = (S - 1) / 2
    order = np.concatenate([np.arange(IMG, S), np.arange(IMG)])
    u = (order - c) / c
    nodes = np.cos(np.pi * (np.arange(NORD) + 0.5) / NORD)
    cheb = np.linalg.inv(orders(nodes).T) @ orders((nodes[:, None] - u[None, :]) / 2)
    cheb[:, 1] /= c
    keys = orders(u)
    keys[1] *= c
    return 4 * cheb, keys


def kernel(**inputs):
    import ml_dtypes
    import numpy as np
    import concourse.bacc as bacc
    from concourse.bass_utils import run_bass_kernel_spmd as run

    i = {k: np.asarray(x) for k, x in inputs.items()}
    f32, bf16 = np.float32, ml_dtypes.bfloat16
    side, patch = 5, 16
    x = i["x"][:, :, :side * patch, :side * patch].reshape(G, NB, 3, side, patch, side, patch)
    x = x.transpose(0, 2, 4, 6, 1, 3, 5).reshape(G, KCONV, P, NB, IMG)
    patches = np.zeros((G, P, KCONV, NB, 32), f32)
    patches[..., :IMG] = x.transpose(0, 2, 1, 3, 4)
    w_conv = i["L0_tok_conv_w"].reshape(D, KCONV, P).transpose(2, 1, 0)
    grid = np.searchsorted(np.arange(1, 32, dtype=f32) / f32(32), np.arange(side, dtype=f32) * f32(0.2), side="right")
    ids = (grid[:, None] * 32 + grid[None, :]).reshape(-1)
    pos = np.zeros((NB, 32, D), f32)
    pos[:, :IMG] = i["L0_tok_pos_table"][ids]
    conv_b = np.zeros((NB, 32, D), f32)
    conv_b[:, :IMG] = i["L0_tok_conv_b"]

    gate = [i["L0_ffn_shared_gate"]] + list(i["L0_ffn_routed_gate"])
    up = [i["L0_ffn_shared_up"]] + list(i["L0_ffn_routed_up"])
    downs = [i["L0_ffn_shared_down"]] + list(i["L0_ffn_routed_down"])
    w = np.zeros((D, WCOLS), f32)
    for n, name in enumerate(("Wq", "Wk", "Wv")):
        w[:, D * n:D * (n + 1)] = i["L0_attn_" + name].T
    w[:, C_R:C_R + 3] = i["L0_ffn_router_w"]
    for e in range(E):
        for c in range(CH):
            at = C_GU + 2 * P * (CH * e + c)
            w[:, at:at + P] = gate[e][:, P * c:P * (c + 1)]
            w[:, at + P:at + 2 * P] = up[e][:, P * c:P * (c + 1)]
    w = np.stack([w[:P], np.concatenate([w[P:], w[P:]])], 1)
    w = w.reshape(P, 2, 8, WPIECE).transpose(2, 0, 1, 3)
    w_down = np.stack([d[P * c:P * (c + 1)] for d in downs for c in range(CH)], 1)
    bqk = np.stack([i["L0_attn_bq"][:96], i["L0_attn_bq"][96:], i["L0_attn_bk"][:96], i["L0_attn_bk"][96:]], 1)

    cheb, keys = chebyshev_tables()
    k_tail = np.zeros((P - BIAS0, HEADS, NB, PAD), bf16)
    kh = keys.astype(f32).astype(bf16)
    rest = keys.astype(f32) - kh.astype(f32)
    km = rest.astype(bf16)
    kl = (rest - km.astype(f32)).astype(bf16)
    rows = [kh, kh, kh, km[2:], km[2:], kl[2:], np.ones((2, S), bf16)]
    k_tail[..., :S] = np.concatenate(rows)[:, None, None, :]

    spread = np.zeros((NB, 32, NB, 4, 32), f32)
    for b in range(NB):
        spread[b, :, b] = np.eye(32, dtype=f32)[:, None, :]

    arrays = {
        "ids": i["x_txt"].reshape(G, NB, TXT).transpose(0, 2, 1),
        "patches": patches.reshape(G, P, KCONV, P),
        "table": i["L0_txt_weight"],
        "w_conv": w_conv,
        "pos": pos.reshape(P, D),
        "conv_b": conv_b.reshape(P, D),
        "bv": np.broadcast_to(i["L0_attn_bv"], (P, D)),
        "bqk": bqk,
        "r_bias": np.broadcast_to(i["L0_ffn_routing_bias"], (P, T, 3)),
        "w_split": w,
        "w_down": w_down,
        "ident": np.eye(P, dtype=f32),
        "spread": spread.reshape(P, NB, P),
        "alpha_t": i["L0_attn_alphas"].T,
        "cheb": cheb.reshape(NORD, NORD * S).astype(f32),
        "k_tail": k_tail.reshape(P - BIAS0, HEADS * COLS),
    }
    arrays = {k: np.ascontiguousarray(x) for k, x in arrays.items()}
    nc = bacc.Bacc("TRN2", target_bir_lowering=False, num_devices=1)
    aps = {k: nc.dram_tensor("in_" + k, x.shape, mybir.dt.from_np(x.dtype), kind="ExternalInput").ap() for k, x in arrays.items()}
    aps["out"] = nc.dram_tensor("out", (B, S, D), F32, kind="ExternalOutput").ap()
    build(nc, aps)
    r = run(nc, [{"in_" + k: x for k, x in arrays.items()}], core_ids=[0])
    return r.results[0]["out"]
```

```python
from contextlib import ExitStack

import concourse.bass as bass
from concourse import mybir

ALU = mybir.AluOpType
ACT = mybir.ActivationFunctionType
F32 = mybir.dt.float32
F32R = mybir.dt.float32r
BF16 = mybir.dt.bfloat16
I32 = mybir.dt.int32
AX = mybir.AxisListType.X

P = 128
B = 32
NB = 4
G = B // NB
TXT = 128
IMG = 25
S = TXT + IMG
PAD = 160
COLS = NB * PAD
T = NB + 1
D = 192
HEADS = 12
HD = D // HEADS
QUADS = HEADS // 4
KCONV = 6
E = 4
CH = 3
EC = E * CH
HALF = COLS // 2
NORD = 6
LEVELS = 1024.0
QMIN, QMAX = -127.0, 126.0
ROUND = 12582912.0
EPS = 1e-5

C_QK, C_V, C_R, C_GU = 0, 2 * D, 3 * D, 3 * D + 4
WCOLS = 3664
WPIECE = WCOLS // 8
PROD_Q = [0, 1, 0, 1, 0, 2]
PROD_K = [0, 0, 1, 1, 2, 0]
BIAS0 = 6 * HD
MAX0 = 126
BIAS_Q2 = [0, 1, 0]


class Count:

    def __init__(self, handle, per):
        self.handle, self.per = handle, per

    def wait(self, eng, g, k=None):
        eng.wait_ge(self.handle, g * self.per + (self.per if k is None else k))


def build(nc, a):
    ctx = ExitStack()
    with ctx:
        def sb(name, shape, dt=F32):
            return ctx.enter_context(nc.sbuf_tensor(name, shape, dt))

        def sem(name):
            return ctx.enter_context(nc.semaphore(name))

        def count(name, per):
            return Count(sem(name), per)

        ps = ctx.enter_context(nc.psum_tensor("ps", [P, 8, 512], F32))
        w_hi = sb("w_hi", [P, 2, WCOLS], F32R)
        w_lo = sb("w_lo", [P, 2, WCOLS], F32R)
        w_down = sb("w_down", [P, EC, D])
        w_conv = sb("w_conv", [P, KCONV, D])
        ident = sb("ident", [P, P])
        pos_bias = sb("pos_bias", [P, D])
        v_bias = sb("v_bias", [P, D])
        qk_bias = sb("qk_bias", [96, 4])
        r_bias = sb("r_bias", [P, T, 3])
        token_ids = sb("token_ids", [P, NB], I32)
        patches = sb("patches", [P, KCONV, P])
        tok = sb("tok", [P, T, D])
        h1 = sb("h1", [P, T, D])
        h2 = sb("h2", [P, T, D])
        xn = sb("xn", [P, T, 2 * P])
        ctx_n = sb("ctx_n", [P, D])
        stats = sb("stats", [P, T, 6])
        mv = sb("mv", [P, T, 2])
        var_eps = sb("var_eps", [P, T])
        rstd = sb("rstd", [P, T])
        minus_half = sb("minus_half", [P, 1])
        eps = sb("eps", [P, 1])
        x1t = sb("x1t", [P, 3, COLS], F32R)
        x2t = sb("x2t", [P, 3, COLS], F32R)
        qk_parts = sb("qk_parts", [96, 4, 3, COLS], BF16)
        q_stack = sb("q_stack", [P, HEADS, COLS], BF16)
        k_stack = sb("k_stack", [P, HEADS, COLS], BF16)
        v_txt = sb("v_txt", [P, NB, HEADS, 32])
        v_img = sb("v_img", [P, NB, HEADS, 32])
        spread = sb("spread", [P, NB, P])
        mx = sb("mx", [P, P])
        NM = NB * HEADS + NB * QUADS
        neg_max = sb("neg_max", [NM, 2, P], BF16)
        hid = sb("hid", [P, EC, COLS])
        flat = hid[:].rearrange("p e c -> p (e c)")
        prob_t = [flat[:, i * 4 * S:(i + 1) * 4 * S].rearrange("p (h c) -> p h c", h=4) for i in range(2)]
        prob_i = [flat[:, (8 + i) * S:(9 + i) * S] for i in range(2)]
        pos_in = flat[:, 3700:3700 + D]
        v_all = flat[:, 4000:4000 + D]
        CT0 = 10 * S + 2
        ctxt = flat[:, CT0:CT0 + NB * QUADS * P].rearrange("p (b t c) -> p b t c", b=NB, t=QUADS)
        w_stage = [flat[:, i * 2 * WPIECE:(i + 1) * 2 * WPIECE].rearrange("p (k c) -> p k c", k=2) for i in range(4)]
        qk_rest_txt = sb("qk_rest_txt", [96, NB, TXT])
        qk_rest_img = sb("qk_rest_img", [96, NB, IMG])
        ctxi = sb("ctxi", [P, QUADS, P])
        rsum = sb("rsum", [P, HEADS])
        th = sb("th", [P, 2, HALF])
        hg = sb("hg", [P, 2, HALF])
        rt = sb("rt", [P, 8, T, 3])
        rs = sb("rs", [P, 2, T])
        alpha_t = sb("alpha_t", [NORD, HEADS])
        cheb = flat[0:NORD, 4600:4600 + NORD * S]
        q_tab = flat[0:HEADS, 5600:5600 + 3 * NORD * S // 2].bitcast(BF16).rearrange("h (i c) -> h i c", i=3)
        q_tab_rest = flat[0:HEADS, 0:NORD * S]

        w_loaded = [sem(f"w_loaded{i}") for i in range(4)]
        w_high, w_split = sem("w_high"), sem("w_split")
        small_loaded, consts_ready, tab_ready, tab_stored = sem("small_loaded"), sem("consts_ready"), sem("tab_ready"), sem("tab_stored")
        tab_mm, tab_part, tables_in, k_tail_in, pos_ready = sem("tab_mm"), sem("tab_part"), sem("tables_in"), sem("k_tail_in"), sem("pos_ready")
        ids_in, patches_in, emb_in = count("ids_in", 16), count("patches_in", 16), count("emb_in", 16 * NB)
        conv_done = count("conv_done", 1)
        quant = count("quant", 2)
        q_a, q_b, clear_done, passed = count("q_a", 1), count("q_b", 1), sem("clear_done"), sem("passed")
        ln_stat, ln_mv, ln_eps, rstd_ready = ([count(f"{n}{k}", T) for k in (1, 2)] for n in ("ln_stat", "ln_mv", "ln_eps", "rstd_ready"))
        tok_kept = count("tok_kept", 1)
        xn1_done, x1t_done, x1_high, x1_split = count("xn1_done", T), count("x1t_done", T), count("x1_high", T), count("x1_split", T)
        xn2_done, x2t_done, x2_high, x2_split = count("xn2_done", T), count("x2t_done", T), count("x2_high", T), count("x2_split", T)
        qk_done, qk_high, qk_sub, qk_mid, qk_low = (count(n, 8) for n in ("qk_done", "qk_high", "qk_sub", "qk_mid", "qk_low"))
        nm_stored = count("nm_stored", 16 * 3)
        parts_stored, stacks_in = count("parts_stored", 64), count("stacks_in", 16 * 12)
        v_mm, v_done = count("v_mm", 2 * NB + 1), count("v_done", 2 * NB + 1)
        s1_done, max_done = count("s1_done", NB * QUADS), count("max_done", NB * QUADS)
        mt_done, nm_high, nm_done, nm_in = count("mt_done", 1), count("nm_high", 1), count("nm_done", 1), count("nm_in", 16 * NB)
        s2t_done, s2_done, exp_done, pv_done, pv_copied = (count(n, NB * QUADS) for n in ("s2t_done", "s2_done", "exp_done", "pv_done", "pv_copied"))
        ct_done, ct_recip, ct_norm, h2_done = count("ct_done", T), count("ct_recip", T), count("ct_norm", T), count("h2_done", T)
        r_mm, r_z, r_exp, r_step, gates_ready = count("r_mm", 1), count("r_z", 1), count("r_exp", 1), count("r_step", 8), count("gates_ready", 1)
        gu_done, tanh_done, hg_done, hid_done = count("gu_done", 4 * EC), count("tanh_done", 2 * EC), count("hg_done", 2 * EC), count("hid_done", 2 * EC)
        down_done, comb_half, comb_done, out_stored = count("down_done", 2 * T), count("comb_half", 2 * T), count("comb_done", 2 * T), count("out_stored", 16 * (1 + NB))

        parts_d = nc.dram_tensor("parts_scratch", (2, 3, D, COLS), BF16).ap()
        nm_d = nc.dram_tensor("neg_max_scratch", (2, NB, HEADS, S), BF16).ap()
        qtab_d = nc.dram_tensor("qtab_scratch", (3, NORD, HEADS, S), BF16).ap()

        QK_BANK = [6, 7]
        GU_BANKS = [(0, 1), (3, 4), (2, 5)]
        CTX_BANK = [6, 6, 6, 6, 7]
        X2_BANK = [7, 7, 7, 6, 7]

        def between(j):
            return {1: [("ctx", 3), ("ctx", 4)], 3: [("norm", 3), ("norm", 4)], 4: [("x2", 3), ("x2", 4)],
                    6: [("router", 0)], 7: [("qk", 0), ("qk", 1)], 8: [("qk", 2), ("qk", 3)],
                    9: [("qk", 4), ("qk", 5)], 10: [("qk", 6), ("qk", 7)], 11: [("keep", 0)]}.get(j, [])

        def among(s):
            b, k = divmod(s - 4, 3)
            return [("ctx", b)] if k == 0 and 0 <= b < 3 else [("norm", b)] if k == 1 and 0 <= b < 3 else \
                [("x2", b)] if k == 2 and 0 <= b < 3 else []

        out_g = a["out"].rearrange("(g b) s d -> g b s d", b=NB)

        def qk_source(i):
            if i % 2 == 0:
                return ps[0:96, QK_BANK[i % 2], 0:NB * TXT].rearrange("p (b c) -> p b c", b=NB)
            return ps[0:96, QK_BANK[i % 2], 0:NB * 32].rearrange("p (b c) -> p b c", b=NB)[:, :, 0:IMG]

        def qk_part(i, k):
            c = slice(0, TXT) if i % 2 == 0 else slice(TXT, S)
            return qk_parts[:, i // 2, k].rearrange("p (b c) -> p b c", b=NB)[:, :, c]

        def qk_rest_of(i):
            return qk_rest_txt[:] if i % 2 == 0 else qk_rest_img[:]

        def pass_waits(eng):
            eng.sem_inc(passed, 1)

        block = ctx.enter_context(nc.Block())

        @block.sync
        def _(sp):
            def load_tokens(n):
                if not (isinstance(n, int) and n == 0):
                    emb_in.wait(sp, n - 1)
                    pass_waits(sp)
                    conv_done.wait(sp, n - 1)
                    pass_waits(sp)
                sp.dma_start(token_ids[:], a["ids"][n]).then_inc(ids_in.handle, 16)
                sp.dma_start(patches[:], a["patches"][n]).then_inc(patches_in.handle, 16)

            def store_parts(n):
                stacks_in.wait(sp, n, 0)
                for t in range(4):
                    qk_low.wait(sp, n, 2 * t + 2)
                    qk_mid.wait(sp, n, 2 * t + 2)
                    r0 = 96 * (t % 2)
                    sp.dma_start(parts_d[t // 2, :, r0:r0 + 96, :].rearrange("s r c -> r s c"),
                                 qk_parts[:, t]).then_inc(parts_stored.handle, 16)

            def load_stacks(n):
                parts_stored.wait(sp, n)
                pass_waits(sp)
                s2_done.wait(sp, n, 0)
                for i in range(6):
                    for qk, stack, parts in ((0, q_stack, PROD_Q), (1, k_stack, PROD_K)):
                        sp.dma_start(stack[HD * i:HD * (i + 1)],
                                     parts_d[qk, parts[i]].rearrange("(h d) c -> d h c", d=HD)
                                     ).then_inc(stacks_in.handle, 16)

            def load_neg_max(n):
                nm_high.wait(sp, n)
                nm_done.wait(sp, n)
                nb = NB * HEADS
                sp.dma_start(nm_d[:, :, :, 0:TXT].rearrange("i b h c -> (b h) i c"), neg_max[0:nb]
                             ).then_inc(nm_stored.handle, 16)
                for i in range(2):
                    sp.dma_start(nm_d[i, :, :, TXT:S].rearrange("b (t q) c -> (b t) q c", q=4),
                                 neg_max[nb:NM, i].rearrange("t (q s) -> t q s", q=4)[:, :, 0:IMG]
                                 ).then_inc(nm_stored.handle, 16)
                nm_stored.wait(sp, n)
                for b in range(NB):
                    sp.dma_start(q_stack[MAX0:P, :, PAD * b:PAD * b + S], nm_d[:, b]).then_inc(nm_in.handle, 16)

            def store_out(n):
                comb_done.wait(sp, n)
                pass_waits(sp)
                sp.dma_start(out_g[n, :, IMG:S, :].rearrange("b s d -> s b d"), h2[:, 0:NB, :]
                             ).then_inc(out_stored.handle, 16)
                for b in range(NB):
                    sp.dma_start(out_g[n, b, 0:IMG, :], h2[32 * b:32 * b + IMG, NB, :]
                                 ).then_inc(out_stored.handle, 16)

            load_tokens(0)
            for i in range(8):
                if i >= 4:
                    sp.wait_ge(w_split, i - 3)
                sp.dma_start(w_stage[i % 4], a["w_split"][i]).then_inc(w_loaded[i % 4], 16)
                if i == 3:
                    sp.dma_start(w_down[:], a["w_down"]).then_inc(small_loaded, 16)
                if i == 0:
                    sp.dma_start(w_conv[:], a["w_conv"]).then_inc(small_loaded, 16)
                    sp.dma_start(ident[:], a["ident"]).then_inc(small_loaded, 16)
                    sp.dma_start(pos_in, a["pos"]).then_inc(small_loaded, 16)
                    sp.dma_start(pos_bias[:], a["conv_b"]).then_inc(small_loaded, 16)
                    sp.dma_start(v_bias[:], a["bv"]).then_inc(small_loaded, 16)
                    sp.dma_start(qk_bias[:], a["bqk"]).then_inc(small_loaded, 16)
                    sp.dma_start(r_bias[:], a["r_bias"]).then_inc(small_loaded, 16)
                    sp.dma_start(alpha_t[:], a["alpha_t"]).then_inc(small_loaded, 16)
                    sp.dma_start(cheb, a["cheb"]).then_inc(small_loaded, 16)
                    sp.dma_start(spread[:], a["spread"]).then_inc(small_loaded, 16)
            sp.wait_ge(consts_ready, 2)
            sp.dma_start(k_stack[BIAS0:P].rearrange("r h c -> r (h c)"), a["k_tail"]).then_inc(k_tail_in, 16)
            sp.wait_ge(tab_ready, 1)
            for i in range(3):
                sp.dma_start(qtab_d[i].rearrange("n h s -> h n s"),
                             q_tab[:, i, :].rearrange("h (n s) -> h n s", n=NORD)).then_inc(tab_stored, 16)
            sp.wait_ge(tab_stored, 48)
            for b in range(NB):
                c0 = PAD * b
                for i in range(3):
                    sp.dma_start(q_stack[BIAS0 + NORD * i:BIAS0 + NORD * (i + 1), :, c0:c0 + S], qtab_d[i]
                                 ).then_inc(tables_in, 16)
                    r = BIAS0 + 3 * NORD + (NORD - 2) * i
                    sp.dma_start(q_stack[r:r + NORD - 2, :, c0:c0 + S], qtab_d[BIAS_Q2[i], 2:NORD]
                                 ).then_inc(tables_in, 16)
            store_parts(0)
            load_stacks(0)

            def group(g, first=False, left=2):
                load_neg_max(g)
                if not first:
                    store_out(g - 1)
                if left > 1:
                    load_tokens(g + 2)
                if left:
                    store_parts(g + 1)
                    load_stacks(g + 1)

            load_tokens(1)
            group(0, first=True)
            with sp.Fori(1, G - 2) as g:
                group(g)
            group(G - 2, left=1)
            group(G - 1, left=0)
            store_out(G - 1)
            out_stored.wait(sp, G - 1)

        @block.gpsimd
        def _(pool):
            nc.gpsimd.memset(eps[:], EPS)
            nc.gpsimd.memset(minus_half[:], -0.5).then_inc(consts_ready, 1)
            pool.wait_ge(consts_ready, 2)

            def gather(n):
                ids_in.wait(pool, n)
                tok_kept.wait(pool, n, 0)
                pass_waits(pool)
                for b in range(NB):
                    nc.gpsimd.indirect_dma_start(
                        out=tok[:, b, :], out_offset=None, in_=a["table"],
                        in_offset=bass.IndirectOffsetOnAxis(ap=token_ids[:, b:b + 1], axis=0),
                    ).then_inc(emb_in.handle, 16)

            def inv_std(n, k, tiles):
                for t in tiles:
                    ln_mv[k].wait(pool, n, t + 1)
                    nc.gpsimd.tensor_tensor(var_eps[:, t:t + 1], mv[:, t, 1:2], eps[:], ALU.add
                                            ).then_inc(ln_eps[k].handle, 1)
                    ln_eps[k].wait(pool, n, t + 1)
                    nc.gpsimd.tensor_tensor(rstd[:, t:t + 1], var_eps[:, t:t + 1], minus_half[:], ALU.pow
                                            ).then_inc(rstd_ready[k].handle, 1)

            def low_parts(n):
                for i in range(8):
                    qk_mid.wait(pool, n, i + 1)
                    nc.gpsimd.tensor_tensor(qk_part(i, 2), qk_rest_of(i), qk_part(i, 1), ALU.subtract
                                            ).then_inc(qk_low.handle, 1)

            gather(0)
            inv_std(0, 0, range(T))
            low_parts(0)
            gather(1)

            def group(g, left=2):
                if left:
                    inv_std(g + 1, 0, range(T))
                inv_std(g, 1, range(T))
                if left:
                    low_parts(g + 1)
                if left > 1:
                    gather(g + 2)

            with pool.Fori(0, G - 2) as g:
                group(g)
            group(G - 2, left=1)
            group(G - 1, left=0)

        @block.scalar
        def _(act):
            def high_x(n, t, done, high, xt, bank):
                done.wait(act, n, t + 1)
                nc.scalar.activation(xt[:, 0:2, P * t:P * (t + 1)],
                                     ps[:, bank, 0:2 * P].rearrange("p (k c) -> p k c", k=2), ACT.Copy
                                     ).then_inc(high.handle, 1)

            def keep_tokens(n):
                if not (isinstance(n, int) and n == 0):
                    h2_done.wait(act, n - 1)
                quant.wait(act, n)
                nc.scalar.activation(h1[:], tok[:], ACT.Copy).then_inc(tok_kept.handle, 1)

            def high_qk(n, i):
                if i == 0:
                    parts_stored.wait(act, n, 0)
                qk_done.wait(act, n, i + 1)
                nc.scalar.activation(qk_part(i, 0), qk_source(i), ACT.Identity, bias=qk_bias[:, i // 2:i // 2 + 1]
                                     ).then_inc(qk_high.handle, 1)

            def exps(g, s):
                bank = 3 * (s % 2)
                s2t_done.wait(act, g, s + 1)
                if s >= 2:
                    pv_done.wait(act, g, s - 1)
                nc.scalar.activation(prob_t[s % 2].rearrange("p (k h) c -> p k (h c)", k=2),
                                     ps[:, bank:bank + 2, 0:2 * S], ACT.Exp, scale=0.25)
                s2_done.wait(act, g, s + 1)
                nc.scalar.activation(prob_i[s % 2], ps[:, 2, 0:S], ACT.Exp, scale=0.25
                                     ).then_inc(exp_done.handle, 1)

            def router_exp(g):
                r_z.wait(act, g)
                nc.scalar.activation(rt[:, 1], rt[:, 0], ACT.Exp, scale=-1.0).then_inc(r_exp.handle, 1)

            def tanh(g, j):
                gu_done.wait(act, g, 2 * j + 1)
                if j >= 2:
                    hg_done.wait(act, g, j - 1)
                nc.scalar.activation(th[:, j % 2], ps[:, GU_BANKS[j % 3][0], 0:HALF], ACT.Tanh, scale=0.5
                                     ).then_inc(tanh_done.handle, 1)

            def neg_high(g):
                mt_done.wait(act, g)
                nc.scalar.activation(neg_max[:, 0], ps[0:NM, 5, 0:P], ACT.Copy, scale=-1.0
                                     ).then_inc(nm_high.handle, 1)

            for i in range(8):
                act.wait_ge(w_loaded[i % 4], 16 * (i // 4 + 1))
                nc.scalar.activation(w_hi[:, :, WPIECE * i:WPIECE * (i + 1)], w_stage[i % 4], ACT.Copy
                                     ).then_inc(w_high, 1)
            act.wait_ge(small_loaded, 176)
            act.wait_ge(consts_ready, 2)
            for t in range(T):
                high_x(0, t, x1t_done, x1_high, x1t, t % 2)
            keep_tokens(0)
            for i in range(8):
                high_qk(0, i)

            def group(g, left=2):
                neg_high(g)
                if left:
                    for t in range(T):
                        high_x(g + 1, t, x1t_done, x1_high, x1t, t % 2)
                for s in range(NB * QUADS + 1):
                    if s < NB * QUADS:
                        exps(g, s)
                    for what, t in among(s):
                        if what == "x2":
                            high_x(g, t, x2t_done, x2_high, x2t, X2_BANK[t])
                for j in range(2 * EC):
                    tanh(g, j)
                    for what, i in between(j):
                        if what == "x2":
                            high_x(g, i, x2t_done, x2_high, x2t, X2_BANK[i])
                        if what == "router":
                            router_exp(g)
                        if what == "qk" and left:
                            high_qk(g + 1, i)
                        if what == "keep" and left:
                            keep_tokens(g + 1)

            with act.Fori(0, G - 1) as g:
                group(g)
            group(G - 1, left=0)

        @block.vector
        def _(dve):
            v = nc.vector

            def quantise(n, step):
                e = tok[:, 0:NB]
                if step == 0:
                    emb_in.wait(dve, n)
                    v.tensor_scalar(e, e, LEVELS, QMIN, ALU.mult, ALU.max).then_inc(q_a.handle, 1)
                if step == 1:
                    q_a.wait(dve, n)
                    v.tensor_scalar(e, e, QMAX, ROUND, ALU.min, ALU.add).then_inc(q_b.handle, 1)
                if step == 2:
                    q_b.wait(dve, n)
                    v.tensor_scalar(e, e, ROUND, 1.0 / LEVELS, ALU.subtract, ALU.mult).then_inc(quant.handle, 1)
                if step == 3:
                    conv_done.wait(dve, n)
                    v.tensor_tensor(tok[:, NB], ps[:, 5, 0:D], pos_bias[:], ALU.add).then_inc(quant.handle, 1)

            def stat(n, k, t, src):
                v.bn_stats(stats[:, t], src[:, t]).then_inc(ln_stat[k].handle, 1)

            def mean_var(n, k, t):
                ln_stat[k].wait(dve, n, t + 1)
                pass_waits(dve)
                v.bn_aggr(mv[:, t], stats[:, t]).then_inc(ln_mv[k].handle, 1)

            def norm(n, k, t, src, done):
                rstd_ready[k].wait(dve, n, t + 1)
                m, r = mv[:, t, 0:1], rstd[:, t:t + 1]
                v.tensor_scalar(xn[:, t, 0:D], src[:, t], m, r, ALU.subtract, ALU.mult)
                v.tensor_scalar(xn[:, t, D:2 * P], src[:, t, P:D], m, r, ALU.subtract, ALU.mult
                                ).then_inc(done.handle, 1)

            def split_x(n, t, high, split, xt, bank):
                high.wait(dve, n, t + 1)
                src, c = ps[:, bank, 0:2 * P], slice(P * t, P * (t + 1))
                v.tensor_tensor(xt[:, 2, c], src[:, 0:P], xt[:, 0, c].bitcast(F32), ALU.subtract)
                v.tensor_tensor(xt[64:P, 1, c], src[64:P, P:2 * P], xt[64:P, 1, c].bitcast(F32), ALU.subtract
                                ).then_inc(split.handle, 1)

            def split_qk(n, i):
                qk_high.wait(dve, n, i + 1)
                if i >= 2:
                    qk_low.wait(dve, n, i - 1)
                v.scalar_tensor_tensor(qk_rest_of(i), qk_source(i), qk_bias[:, i // 2:i // 2 + 1], qk_part(i, 0),
                                       ALU.add, ALU.subtract).then_inc(qk_sub.handle, 1)
                qk_sub.wait(dve, n, i + 1)
                v.tensor_copy(qk_part(i, 1), qk_rest_of(i)).then_inc(qk_mid.handle, 1)

            def values(g):
                v_mm.wait(dve, g, 1)
                v.tensor_tensor(v_all, ps[:, 7, 0:D], v_bias[:], ALU.add).then_inc(v_done.handle, 1)
                for b in range(NB):
                    v_mm.wait(dve, g, 2 * b + 2)
                    v.tensor_tensor(v_txt[:, b, :, 0:HD], ps[:, 6, 0:D].rearrange("p (h d) -> p h d", d=HD),
                                    v_bias[:].rearrange("p (h d) -> p h d", d=HD), ALU.add
                                    ).then_inc(v_done.handle, 1)
                    v_mm.wait(dve, g, 2 * b + 3)
                    for q in range(4):
                        rows = slice(32 * q, 32 * q + IMG)
                        ins = v.tensor_copy(v_img[rows, b].rearrange("p (t q) d -> p q t d", q=4)[:, q, :, 0:HD],
                                            ps[rows, 7, 0:D].rearrange("p (t q d) -> p q t d", q=4, d=HD)[:, q])
                    ins.then_inc(v_done.handle, 1)

            def maxima(g, s):
                b, t = s // QUADS, s % QUADS
                s1_done.wait(dve, g, s + 1)
                c = HEADS * b + 4 * t
                v.tensor_reduce(mx[:, c:c + 4].rearrange("p (k h) -> p k h", k=2),
                                ps[:, 0:2, 0:2 * S].rearrange("p k (h c) -> p k h c", h=2), AX, ALU.max)
                c = NB * HEADS + QUADS * b + t
                v.tensor_reduce(mx[:, c:c + 1], ps[:, 2, 0:S], AX, ALU.max).then_inc(max_done.handle, 1)

            def neg_low(g):
                nm_high.wait(dve, g)
                v.scalar_tensor_tensor(neg_max[:, 1], ps[0:NM, 5, 0:P], -1.0, neg_max[:, 0],
                                       ALU.mult, ALU.subtract).then_inc(nm_done.handle, 1)

            def copy_ctx(g, s):
                b, t = s // QUADS, s % QUADS
                pv_done.wait(dve, g, s + 1)
                v.tensor_copy(ctxt[:, b, t], ps[:, 5, 0:TXT])
                v.tensor_copy(ctxi[:, t, 32 * b:32 * b + IMG], ps[:, 5, TXT:S]).then_inc(pv_copied.handle, 1)

            def add_ctx(g, t):
                if t == 0:
                    out_stored.wait(dve, g, 0)
                c = ps[:, CTX_BANK[t], 0:HEADS * 32].rearrange("p (h d) -> p h d", d=32)
                ct_done.wait(dve, g, t + 1)
                v.reciprocal(rsum[:], c[:, :, HD]).then_inc(ct_recip.handle, 1)
                ct_recip.wait(dve, g, t + 1)
                v.tensor_tensor(ctx_n[:].rearrange("p (h d) -> p h d", d=HD), c[:, :, 0:HD],
                                rsum[:].unsqueeze(2).broadcast_to([P, HEADS, HD]), ALU.mult
                                ).then_inc(ct_norm.handle, 1)
                ct_norm.wait(dve, g, t + 1)
                v.tensor_tensor(h2[:, t], ctx_n[:], h1[:, t], ALU.add).then_inc(h2_done.handle, 1)
                h2_done.wait(dve, g, t + 1)
                stat(g, 1, t, h2)
                mean_var(g, 1, t)

            def gates(g):
                step = [0]

                def then(ins):
                    step[0] += 1
                    ins.then_inc(r_step.handle, 1)
                    r_step.wait(dve, g, step[0])

                z, e, p, keep, w, tmp = rt[:, 0], rt[:, 1], rt[:, 2], rt[:, 3], rt[:, 4], rt[:, 5]
                r_mm.wait(dve, g)
                v.tensor_tensor(z, ps[:, 6, 0:4 * T].rearrange("p (t e) -> p t e", e=4)[:, :, 0:3], r_bias[:], ALU.add
                                ).then_inc(r_z.handle, 1)
                r_exp.wait(dve, g)
                then(v.tensor_scalar(e, e, 1.0, None, ALU.add))
                then(v.reciprocal(p, e))
                v.tensor_tensor(tmp[:, :, 0], p[:, :, 0], p[:, :, 1], ALU.is_ge)
                v.tensor_tensor(tmp[:, :, 1], p[:, :, 0], p[:, :, 2], ALU.is_ge)
                then(v.tensor_tensor(tmp[:, :, 2], p[:, :, 1], p[:, :, 2], ALU.is_ge))
                v.tensor_tensor(keep[:, :, 0], tmp[:, :, 0], tmp[:, :, 1], ALU.max)
                v.tensor_tensor(keep[:, :, 2], tmp[:, :, 1], tmp[:, :, 2], ALU.min)
                then(v.tensor_scalar(rt[:, 6, :, 0], tmp[:, :, 0], -1.0, 1.0, ALU.mult, ALU.add))
                v.tensor_tensor(keep[:, :, 1], rt[:, 6, :, 0], tmp[:, :, 2], ALU.max)
                then(v.tensor_scalar(keep[:, :, 2], keep[:, :, 2], -1.0, 1.0, ALU.mult, ALU.add))
                then(v.tensor_tensor(w, keep, p, ALU.mult))
                then(v.tensor_reduce(rs[:, 0], w, AX, ALU.add))
                then(v.reciprocal(rs[:, 1], rs[:, 0]))
                v.scalar_tensor_tensor(rt[:, 7], w, 0.5, rs[:, 1].unsqueeze(2).broadcast_to([P, T, 3]),
                                       ALU.mult, ALU.mult).then_inc(gates_ready.handle, 1)

            def hidden(g, j):
                hf, ec = j // EC, j % EC
                bg, bu = GU_BANKS[j % 3]
                tanh_done.wait(dve, g, j + 1)
                v.scalar_tensor_tensor(hg[:, j % 2], th[:, j % 2], 1.0, ps[:, bg, 0:HALF], ALU.add, ALU.mult
                                       ).then_inc(hg_done.handle, 1)
                hg_done.wait(dve, g, j + 1)
                gu_done.wait(dve, g, 2 * j + 2)
                v.tensor_tensor(hid[:, ec, HALF * hf:HALF * (hf + 1)], hg[:, j % 2], ps[:, bu, 0:HALF], ALU.mult
                                ).then_inc(hid_done.handle, 1)

            def combine(n, i):
                t, pr = i // 2, i % 2
                down_done.wait(dve, n, i + 1)
                if pr:
                    comb_done.wait(dve, n, i)
                for k in range(2):
                    gate = 0.5 if (pr, k) == (0, 0) else rt[:, 7, t, 2 * pr + k - 1:2 * pr + k]
                    v.scalar_tensor_tensor(h2[:, t], ps[:, 3 + pr, D * k:D * (k + 1)], gate, h2[:, t],
                                           ALU.mult, ALU.add).then_inc((comb_done if k else comb_half).handle, 1)
                    if not k:
                        comb_half.wait(dve, n, i + 1)

            v.memset(qk_parts[:], 0.0)
            v.memset(mx[:], 0.0)
            v.memset(q_stack[64:P].rearrange("p h c -> p (h c)"), 0.0)
            v.memset(v_txt[:], 0.0)
            v.memset(v_img[:], 0.0)
            v.memset(ctxi[:], 1.0).then_inc(clear_done, 1)
            dve.wait_ge(clear_done, 1)
            v.memset(v_txt[:, :, :, HD:HD + 1], 1.0)
            for q in range(4):
                rows = slice(32 * q, 32 * q + IMG)
                ins = v.memset(v_img[rows].rearrange("p b (t q) d -> p q (b t) d", q=4)[:, q, :, HD:HD + 1], 1.0)
            ins.then_inc(consts_ready, 1)
            dve.wait_ge(consts_ready, 2)
            dve.wait_ge(small_loaded, 176)
            v.tensor_tensor(pos_bias[:], pos_bias[:], pos_in, ALU.add).then_inc(pos_ready, 1)
            for i in range(8):
                dve.wait_ge(w_high, i + 1)
                c = slice(WPIECE * i, WPIECE * (i + 1))
                v.tensor_tensor(w_lo[:, :, c], w_stage[i % 4], w_hi[:, :, c].bitcast(F32), ALU.subtract
                                ).then_inc(w_split, 1)
            dve.wait_ge(tab_mm, 1)
            tab = ps[0:HEADS, 6:8, 0:NORD * S // 2]
            part = [q_tab[:, i].rearrange("h (k c) -> h k c", k=2) for i in range(3)]
            rest = q_tab_rest.rearrange("h (k c) -> h k c", k=2)
            v.tensor_copy(part[0], tab).then_inc(tab_part, 1)
            dve.wait_ge(tab_part, 1)
            dve.wait_ge(w_split, 8)
            v.tensor_tensor(rest, tab, part[0], ALU.subtract).then_inc(tab_part, 1)
            dve.wait_ge(tab_part, 2)
            v.tensor_copy(part[1], rest).then_inc(tab_part, 1)
            dve.wait_ge(tab_part, 3)
            v.tensor_tensor(part[2], rest, part[1], ALU.subtract).then_inc(tab_ready, 1)
            dve.wait_ge(pos_ready, 1)

            for k in range(4):
                quantise(0, k)
            quant.wait(dve, 0)
            for t in range(T):
                stat(0, 0, t, tok)
            for t in range(T):
                mean_var(0, 0, t)
            for t in range(T):
                norm(0, 0, t, tok, xn1_done)
            for t in range(T):
                split_x(0, t, x1_high, x1_split, x1t, t % 2)
            for i in range(8):
                split_qk(0, i)

            def next_tokens(n, s):
                if s < 4:
                    quantise(n, s)
                if 4 <= s < 4 + T:
                    if s == 4:
                        quant.wait(dve, n)
                    stat(n, 0, s - 4, tok)
                if 5 <= s < 5 + T:
                    mean_var(n, 0, s - 5)
                if 7 <= s < 7 + T:
                    norm(n, 0, s - 7, tok, xn1_done)

            def group(g, first=False, left=2):
                for s in range(NB * QUADS):
                    maxima(g, s)
                    if not first and s < 2 * T:
                        combine(g - 1, s)
                    if left:
                        next_tokens(g + 1, s)
                neg_low(g)
                values(g)
                if left:
                    for t in range(T):
                        split_x(g + 1, t, x1_high, x1_split, x1t, t % 2)
                for s in range(NB * QUADS + 1):
                    if s:
                        copy_ctx(g, s - 1)
                    for what, t in among(s):
                        if what == "ctx":
                            add_ctx(g, t)
                        if what == "norm":
                            norm(g, 1, t, h2, xn2_done)
                        if what == "x2":
                            split_x(g, t, x2_high, x2_split, x2t, X2_BANK[t])
                for j in range(2 * EC):
                    hidden(g, j)
                    for what, i in between(j):
                        if what == "ctx":
                            add_ctx(g, i)
                        if what == "norm":
                            norm(g, 1, i, h2, xn2_done)
                        if what == "x2":
                            split_x(g, i, x2_high, x2_split, x2t, X2_BANK[i])
                        if what == "router":
                            gates(g)
                        if what == "qk" and left:
                            split_qk(g + 1, i)

            group(0, first=True)
            with dve.Fori(1, G - 1) as g:
                group(g)
            group(G - 1, left=0)
            for s in range(2 * T):
                combine(G - 1, s)

        @block.tensor
        def _(pe):
            mm = nc.tensor.matmul

            def split_mm(out, w, x, lhs_is_x):
                passes = ((w_hi, 0, 0), (w_hi, 0, 2), (w_lo, 0, 0), (w_hi, 1, 1), (w_lo, 1, 1))
                for i, (wt, wk, xk) in enumerate(passes):
                    l, r = wt[:, wk, w], x(xk)
                    if lhs_is_x:
                        l, r = r, l
                    ins = mm(out, l, r, start=(i == 0), stop=(i == 4))
                return ins

            def conv(n):
                patches_in.wait(pe, n)
                for c in range(KCONV):
                    ins = mm(ps[:, 5, 0:D], patches[:, c], w_conv[:, c], start=(c == 0), stop=(c == KCONV - 1))
                ins.then_inc(conv_done.handle, 1)

            def turn(n, t, xn_done, done, bank):
                xn_done.wait(pe, n, t + 1)
                nc.tensor.transpose(ps[:, bank, 0:P], xn[:, t, 0:P], ident[:])
                nc.tensor.transpose(ps[:, bank, P:2 * P], xn[:, t, P:2 * P], ident[:]).then_inc(done.handle, 1)

            def turn_x1(n):
                for t in range(T):
                    if t >= 2:
                        x1_split.wait(pe, n, t - 1)
                    turn(n, t, xn1_done, x1t_done, t % 2)

            def qk(n, i):
                c = slice(0, NB * TXT) if i % 2 == 0 else slice(NB * TXT, T * P)
                at = C_QK + 96 * (i // 2)
                if i >= 2:
                    qk_sub.wait(pe, n, i - 1)
                split_mm(ps[0:96, QK_BANK[i % 2], 0:c.stop - c.start], slice(at, at + 96),
                         lambda k: x1t[:, k, c], False).then_inc(qk_done.handle, 1)

            def values(g):
                img = slice(NB * TXT, T * P)
                split_mm(ps[:, 7, 0:D], slice(C_V, C_V + D), lambda k: x1t[:, k, img], True).then_inc(v_mm.handle, 1)
                for b in range(NB):
                    if b:
                        v_done.wait(pe, g, 2 * b)
                    split_mm(ps[:, 6, 0:D], slice(C_V, C_V + D), lambda k: x1t[:, k, P * b:P * (b + 1)], True
                             ).then_inc(v_mm.handle, 1)
                    v_done.wait(pe, g, 2 * b + 1)
                    mm(ps[:, 7, 0:D], spread[:, b], v_all, start=True, stop=True).then_inc(v_mm.handle, 1)

            def scores_by_query(g, s):
                b, t = s // QUADS, s % QUADS
                if s:
                    max_done.wait(pe, g, s)
                c = PAD * b
                for i in range(4):
                    mm(ps[:, i // 2, S * (i % 2):S * (i % 2 + 1)], q_stack[0:MAX0, 4 * t + i, c:c + TXT],
                       k_stack[0:MAX0, 4 * t + i, c:c + S], start=True, stop=True)
                for i in range(4):
                    ins = mm(ps[32 * i:32 * i + 32, 2, 0:S], q_stack[0:MAX0, 4 * t + i, c + TXT:c + PAD],
                             k_stack[0:MAX0, 4 * t + i, c:c + S], start=True, stop=True)
                ins.then_inc(s1_done.handle, 1)

            def scores_txt_keys(g, s):
                b, t = s // QUADS, s % QUADS
                if s >= 2:
                    exp_done.wait(pe, g, s - 1)
                c, bank = PAD * b, 3 * (s % 2)
                for i in range(4):
                    ins = mm(ps[:, bank + i // 2, S * (i % 2):S * (i % 2 + 1)], k_stack[:, 4 * t + i, c:c + TXT],
                             q_stack[:, 4 * t + i, c:c + S], start=True, stop=True)
                ins.then_inc(s2t_done.handle, 1)

            def scores_img_keys(g, s):
                b, t = s // QUADS, s % QUADS
                c = PAD * b
                if s:
                    exp_done.wait(pe, g, s)
                for i in range(4):
                    ins = mm(ps[32 * i:32 * i + 32, 2, 0:S], k_stack[:, 4 * t + i, c + TXT:c + PAD],
                             q_stack[:, 4 * t + i, c:c + S], start=True, stop=True)
                ins.then_inc(s2_done.handle, 1)

            def context(g, s):
                b, t = s // QUADS, s % QUADS
                exp_done.wait(pe, g, s + 1)
                if s:
                    pv_copied.wait(pe, g, s)
                mm(ps[:, 5, 0:S], v_img[:, b, 4 * t:4 * t + 4].rearrange("p h d -> p (h d)"), prob_i[s % 2],
                   start=True, stop=False)
                for i in range(4):
                    ins = mm(ps[32 * i:32 * i + 32, 5, 0:S], v_txt[:, b, 4 * t + i], prob_t[s % 2][:, i],
                             start=False, stop=True)
                ins.then_inc(pv_done.handle, 1)

            def turn_ctx(g, t):
                pv_copied.wait(pe, g, QUADS * min(t + 1, NB))
                if t == NB:
                    x2_split.wait(pe, g, 3)
                elif t:
                    h2_done.wait(pe, g, t)
                for k in range(QUADS):
                    src = ctxt[:, t, k] if t < NB else ctxi[:, k]
                    ins = nc.tensor.transpose(ps[:, CTX_BANK[t], P * k:P * (k + 1)], src, ident[:])
                ins.then_inc(ct_done.handle, 1)

            def turn_x2(g, t):
                if 0 < t < 3:
                    x2_split.wait(pe, g, t)
                turn(g, t, xn2_done, x2t_done, X2_BANK[t])

            def router(g):
                x2_split.wait(pe, g)
                for t in range(T):
                    ins = split_mm(ps[:, 6, 4 * t:4 * t + 4], slice(C_R, C_R + 4),
                                   lambda k: x2t[:, k, P * t:P * (t + 1)], True)
                ins.then_inc(r_mm.handle, 1)

            def gate_up(g, j):
                hf, ec = j // EC, j % EC
                if j == 0:
                    x2_split.wait(pe, g, 3)
                if j == EC:
                    x2_split.wait(pe, g)
                if j >= 3:
                    hid_done.wait(pe, g, j - 2)
                for k in range(2):
                    c = C_GU + 2 * P * ec + P * k
                    split_mm(ps[:, GU_BANKS[j % 3][k], 0:HALF], slice(c, c + P),
                             lambda x: x2t[:, x, HALF * hf:HALF * (hf + 1)], False).then_inc(gu_done.handle, 1)

            def down(n, i):
                t, pr = i // 2, i % 2
                if i == 0:
                    hid_done.wait(pe, n)
                if i >= 2:
                    comb_done.wait(pe, n, i - 1)
                for k in range(2):
                    for c in range(CH):
                        ec = CH * (2 * pr + k) + c
                        ins = mm(ps[:, 3 + pr, D * k:D * (k + 1)], hid[:, ec, P * t:P * (t + 1)], w_down[:, ec],
                                 start=(c == 0), stop=(c == CH - 1))
                ins.then_inc(down_done.handle, 1)

            pe.wait_ge(small_loaded, 176)
            pe.wait_ge(w_split, 8)
            for i in range(2):
                n = NORD * S // 2
                ins = mm(ps[0:HEADS, 6 + i, 0:n], alpha_t[:], cheb[:, n * i:n * (i + 1)], start=True, stop=True)
            ins.then_inc(tab_mm, 1)
            conv(0)
            turn_x1(0)
            pe.wait_ge(tab_ready, 1)
            x1_split.wait(pe, 0)
            for i in range(8):
                qk(0, i)
            pe.wait_ge(tables_in, 16 * 6 * NB)
            pe.wait_ge(k_tail_in, 16)
            pe.wait_ge(consts_ready, 2)

            def group(g, first=False, left=2):
                stacks_in.wait(pe, g)
                if not first:
                    hid_done.wait(pe, g - 1)
                if left:
                    conv(g + 1)
                for s in range(NB * QUADS):
                    scores_by_query(g, s)
                    if not first and s < 2 * T:
                        down(g - 1, s)
                max_done.wait(pe, g)
                if left:
                    quant.wait(pe, g + 1)
                nc.tensor.transpose(ps[:, 5, 0:P], mx[:], ident[:]).then_inc(mt_done.handle, 1)
                values(g)
                if left:
                    turn_x1(g + 1)
                if not first:
                    comb_done.wait(pe, g - 1)
                if left:
                    x1_split.wait(pe, g + 1)
                v_done.wait(pe, g)
                nm_in.wait(pe, g)
                for s in range(NB * QUADS + 1):
                    if s < NB * QUADS:
                        scores_txt_keys(g, s)
                        scores_img_keys(g, s)
                    if s:
                        context(g, s - 1)
                    for what, t in among(s):
                        if what == "ctx":
                            turn_ctx(g, t)
                        if what == "x2":
                            turn_x2(g, t)
                for j in range(2 * EC):
                    gate_up(g, j)
                    for what, i in between(j):
                        if what == "ctx":
                            turn_ctx(g, i)
                        if what == "x2":
                            turn_x2(g, i)
                        if what == "router":
                            router(g)
                        if what == "qk" and left:
                            if i == 0:
                                r_z.wait(pe, g)
                            qk(g + 1, i)

            group(0, first=True)
            with pe.Fori(1, G - 1) as g:
                group(g)
            group(G - 1, left=0)
            for s in range(2 * T):
                down(G - 1, s)


def chebyshev_tables():
    import numpy as np

    def orders(x):
        t = [np.ones_like(x), x]
        while len(t) < NORD:
            t.append(2 * x * t[-1] - t[-2])
        return np.stack(t)

    c = (S - 1) / 2
    order = np.concatenate([np.arange(IMG, S), np.arange(IMG)])
    u = (order - c) / c
    nodes = np.cos(np.pi * (np.arange(NORD) + 0.5) / NORD)
    cheb = np.linalg.inv(orders(nodes).T) @ orders((nodes[:, None] - u[None, :]) / 2)
    cheb[:, 1] /= c
    keys = orders(u)
    keys[1] *= c
    return 4 * cheb, keys


def kernel(**inputs):
    import ml_dtypes
    import numpy as np
    import concourse.bacc as bacc
    from concourse.bass_utils import run_bass_kernel_spmd as run

    i = {k: np.asarray(x) for k, x in inputs.items()}
    f32, bf16 = np.float32, ml_dtypes.bfloat16
    side, patch = 5, 16
    x = i["x"][:, :, :side * patch, :side * patch].reshape(G, NB, 3, side, patch, side, patch)
    x = x.transpose(0, 2, 4, 6, 1, 3, 5).reshape(G, KCONV, P, NB, IMG)
    patches = np.zeros((G, P, KCONV, NB, 32), f32)
    patches[..., :IMG] = x.transpose(0, 2, 1, 3, 4)
    w_conv = i["L0_tok_conv_w"].reshape(D, KCONV, P).transpose(2, 1, 0)
    grid = np.searchsorted(np.arange(1, 32, dtype=f32) / f32(32), np.arange(side, dtype=f32) * f32(0.2), side="right")
    ids = (grid[:, None] * 32 + grid[None, :]).reshape(-1)
    pos = np.zeros((NB, 32, D), f32)
    pos[:, :IMG] = i["L0_tok_pos_table"][ids]
    conv_b = np.zeros((NB, 32, D), f32)
    conv_b[:, :IMG] = i["L0_tok_conv_b"]

    gate = [i["L0_ffn_shared_gate"]] + list(i["L0_ffn_routed_gate"])
    up = [i["L0_ffn_shared_up"]] + list(i["L0_ffn_routed_up"])
    downs = [i["L0_ffn_shared_down"]] + list(i["L0_ffn_routed_down"])
    w = np.zeros((D, WCOLS), f32)
    for n, name in enumerate(("Wq", "Wk", "Wv")):
        w[:, D * n:D * (n + 1)] = i["L0_attn_" + name].T
    w[:, C_R:C_R + 3] = i["L0_ffn_router_w"]
    for e in range(E):
        for c in range(CH):
            at = C_GU + 2 * P * (CH * e + c)
            w[:, at:at + P] = gate[e][:, P * c:P * (c + 1)]
            w[:, at + P:at + 2 * P] = up[e][:, P * c:P * (c + 1)]
    w = np.stack([w[:P], np.concatenate([w[P:], w[P:]])], 1)
    w = w.reshape(P, 2, 8, WPIECE).transpose(2, 0, 1, 3)
    w_down = np.stack([d[P * c:P * (c + 1)] for d in downs for c in range(CH)], 1)
    bqk = np.stack([i["L0_attn_bq"][:96], i["L0_attn_bq"][96:], i["L0_attn_bk"][:96], i["L0_attn_bk"][96:]], 1)

    cheb, keys = chebyshev_tables()
    k_tail = np.zeros((P - BIAS0, HEADS, NB, PAD), bf16)
    kh = keys.astype(f32).astype(bf16)
    rest = keys.astype(f32) - kh.astype(f32)
    km = rest.astype(bf16)
    kl = (rest - km.astype(f32)).astype(bf16)
    rows = [kh, kh, kh, km[2:], km[2:], kl[2:], np.ones((2, S), bf16)]
    k_tail[..., :S] = np.concatenate(rows)[:, None, None, :]

    spread = np.zeros((NB, 32, NB, 4, 32), f32)
    for b in range(NB):
        spread[b, :, b] = np.eye(32, dtype=f32)[:, None, :]

    arrays = {
        "ids": i["x_txt"].reshape(G, NB, TXT).transpose(0, 2, 1),
        "patches": patches.reshape(G, P, KCONV, P),
        "table": i["L0_txt_weight"],
        "w_conv": w_conv,
        "pos": pos.reshape(P, D),
        "conv_b": conv_b.reshape(P, D),
        "bv": np.broadcast_to(i["L0_attn_bv"], (P, D)),
        "bqk": bqk,
        "r_bias": np.broadcast_to(i["L0_ffn_routing_bias"], (P, T, 3)),
        "w_split": w,
        "w_down": w_down,
        "ident": np.eye(P, dtype=f32),
        "spread": spread.reshape(P, NB, P),
        "alpha_t": i["L0_attn_alphas"].T,
        "cheb": cheb.reshape(NORD, NORD * S).astype(f32),
        "k_tail": k_tail.reshape(P - BIAS0, HEADS * COLS),
    }
    arrays = {k: np.ascontiguousarray(x) for k, x in arrays.items()}
    nc = bacc.Bacc("TRN2", target_bir_lowering=False, num_devices=1)
    aps = {k: nc.dram_tensor("in_" + k, x.shape, mybir.dt.from_np(x.dtype), kind="ExternalInput").ap() for k, x in arrays.items()}
    aps["out"] = nc.dram_tensor("out", (B, S, D), F32, kind="ExternalOutput").ap()
    build(nc, aps)
    r = run(nc, [{"in_" + k: x for k, x in arrays.items()}], core_ids=[0])
    return r.results[0]["out"]
```

```python
from contextlib import ExitStack

import concourse.bass as bass
from concourse import mybir

ALU = mybir.AluOpType
ACT = mybir.ActivationFunctionType
F32 = mybir.dt.float32
F32R = mybir.dt.float32r
BF16 = mybir.dt.bfloat16
I32 = mybir.dt.int32
AX = mybir.AxisListType.X

P = 128
B = 32
NB = 4
G = B // NB
TXT = 128
IMG = 25
S = TXT + IMG
PAD = 160
COLS = NB * PAD
T = NB + 1
D = 192
HEADS = 12
HD = D // HEADS
QUADS = HEADS // 4
KCONV = 6
QKC = 2 * D // P
E = 4
CH = 3
EC = E * CH
HALF = COLS // 2
NORD = 6
LEVELS = 1024.0
QMIN, QMAX = -127.0, 126.0
ROUND = 12582912.0
EPS = 1e-5

C_QK, C_V, C_R, C_GU = 0, 2 * D, 3 * D, 3 * D + 4
WCOLS = 3664
WPIECE = WCOLS // 8
PROD_Q = [0, 1, 0, 1, 2, 0]
PROD_K = [0, 1, 1, 0, 0, 2]
BIAS0 = 6 * HD
MAX0 = 126
BIAS_Q2 = [0, 1, 0]


class Count:

    def __init__(self, handle, per):
        self.handle, self.per = handle, per

    def wait(self, eng, g, k=None):
        eng.wait_ge(self.handle, g * self.per + (self.per if k is None else k))


def build(nc, a):
    ctx = ExitStack()
    with ctx:
        def sb(name, shape, dt=F32):
            return ctx.enter_context(nc.sbuf_tensor(name, shape, dt))

        def sem(name):
            return ctx.enter_context(nc.semaphore(name))

        def count(name, per):
            return Count(sem(name), per)

        ps = ctx.enter_context(nc.psum_tensor("ps", [P, 8, 512], F32))
        w_hi = sb("w_hi", [P, 2, WCOLS], F32R)
        w_lo = sb("w_lo", [P, 2, WCOLS], F32R)
        w_down = sb("w_down", [P, EC, D])
        w_conv = sb("w_conv", [P, KCONV, D])
        ident = sb("ident", [P, P])
        pos_bias = sb("pos_bias", [P, D])
        v_bias = sb("v_bias", [P, D])
        qk_bias = sb("qk_bias", [P, QKC])
        r_bias = sb("r_bias", [P, T, 3])
        token_ids = sb("token_ids", [P, NB], I32)
        patches = sb("patches", [P, KCONV, P])
        tok = sb("tok", [P, T, D])
        h1 = sb("h1", [P, T, D])
        h2 = sb("h2", [P, T, D])
        xn = [sb(f"xn{i}", [P, T, 2 * P]) for i in (1, 2)]
        ctx_n = sb("ctx_n", [P, D])
        v_all = ctx_n[:]
        stats = sb("stats", [P, 2, T, 6])
        mv = sb("mv", [P, 2, T, 2])
        var_eps = sb("var_eps", [P, 2, T])
        rstd = sb("rstd", [P, 2, T])
        minus_half = sb("minus_half", [P, T])
        eps = sb("eps", [P, T])
        x1t = sb("x1t", [P, 3, COLS], F32R)
        x2t = sb("x2t", [P, 3, COLS], F32R)
        qk_parts = sb("qk_parts", [P, QKC, 3, COLS], BF16)
        q_stack = sb("q_stack", [P, HEADS, COLS], BF16)
        k_stack = sb("k_stack", [P, HEADS, COLS], BF16)
        v_txt = sb("v_txt", [P, NB, HEADS, 32])
        v_img = sb("v_img", [P, NB, QUADS, 32])
        pick = sb("pick", [P, NB, 32])
        mx = sb("mx", [P, P])
        NM = NB * HEADS + NB * QUADS
        neg_max = sb("neg_max", [NM, 2, P], BF16)
        hid = sb("hid", [P, EC, COLS])
        flat = hid[:].rearrange("p e c -> p (e c)")
        prob_t = [flat[:, i * 4 * S:(i + 1) * 4 * S].rearrange("p (h c) -> p h c", h=4) for i in range(2)]
        prob_i = [flat[:, (8 + i) * S:(9 + i) * S] for i in range(2)]
        pos_in = flat[:, 3700:3700 + D]
        CT0 = EC // 2 * COLS - NB * QUADS * P
        ctxt = flat[:, CT0:CT0 + NB * QUADS * P].rearrange("p (b t c) -> p b t c", b=NB, t=QUADS)
        w_stage = [flat[:, i * 2 * WPIECE:(i + 1) * 2 * WPIECE].rearrange("p (k c) -> p k c", k=2) for i in range(4)]
        qk_rest_txt = sb("qk_rest_txt", [P, NB, TXT])
        qk_rest_img = sb("qk_rest_img", [P, NB, IMG])
        ctxi = sb("ctxi", [P, QUADS, P])
        rsum = sb("rsum", [P, HEADS])
        th = sb("th", [P, 2, HALF])
        hg = sb("hg", [P, 2, HALF])
        rt = sb("rt", [P, 8, T, 3])
        logits = sb("logits", [4, T * P])
        alpha_t = flat[0:NORD, 4580:4580 + HEADS]
        cheb = flat[0:NORD, 4600:4600 + NORD * S]
        q_tab = flat[0:HEADS, 5600:5600 + 3 * NORD * PAD // 2].bitcast(BF16).rearrange("h (n c) -> h n c", c=PAD)
        q_tab_rest = h2[0:HEADS].rearrange("h t d -> h (t d)")[:, 0:NORD * S]

        w_loaded = [sem(f"w_loaded{i}") for i in range(4)]
        w_high, w_split = sem("w_high"), sem("w_split")
        small_loaded, late_loaded, down_loaded = sem("small_loaded"), sem("late_loaded"), sem("down_loaded")
        clear_done, consts_ready, eps_ready, pos_ready = sem("clear_done"), sem("consts_ready"), sem("eps_ready"), sem("pos_ready")
        tab_loaded, tab_mm, tab_part, tab_ready = sem("tab_loaded"), sem("tab_mm"), sem("tab_part"), sem("tab_ready")
        tab_stored, tables_in, k_tail_in, passed = sem("tab_stored"), sem("tables_in"), sem("k_tail_in"), sem("passed")
        ids_in, patches_in, emb_in = count("ids_in", 16), count("patches_in", 16), count("emb_in", 16 * NB)
        conv_done = count("conv_done", 1)
        quant, img_tokens = count("quant", 1), count("img_tokens", 1)
        q_a, q_b = count("q_a", 1), count("q_b", 1)
        ln_stat, ln_mv, ln_eps, rstd_ready = ([count(f"{n}{k}", T) for k in (1, 2)] for n in ("ln_stat", "ln_mv", "ln_eps", "rstd_ready"))
        tok_kept, v_biased = count("tok_kept", 1), count("v_biased", 1)
        xn1_normed = count("xn1_normed", T)
        xn1_done, x1t_done, x1_high, x1_split = count("xn1_done", T), count("x1t_done", T), count("x1_high", T), count("x1_split", T)
        xn2_done, x2t_done, x2_high, x2_split = count("xn2_done", T), count("x2t_done", T), count("x2_high", T), count("x2_split", T)
        qk_done, qk_high, qk_sub, qk_mid, qk_low = (count(n, 2 * QKC) for n in ("qk_done", "qk_high", "qk_sub", "qk_mid", "qk_low"))
        nm_stored = count("nm_stored", 16 * 3)
        parts_stored, stacks_in = count("parts_stored", 16 * 4), count("stacks_in", 16 * 9)
        v_mm, v_all_done, v_txt_done = count("v_mm", NB + 1), count("v_all_done", 1), count("v_txt_done", NB)
        v_img_mm, v_img_done = count("v_img_mm", 1), count("v_img_done", 1)
        s1_done, max_done = count("s1_done", NB * QUADS), count("max_done", NB * QUADS)
        mt_done, nm_high, nm_done = count("mt_done", 1), count("nm_high", 1), count("nm_done", 1)
        nm_in = [count(f"nm_in{b}", 16) for b in range(NB)]
        s2_done, exp_done, pv_done, pv_copied = (count(n, NB * QUADS) for n in ("s2_done", "exp_done", "pv_done", "pv_copied"))
        ct_done, ct_recip, ct_norm, added = count("ct_done", T), count("ct_recip", T), count("ct_norm", T), count("added", T)
        r_copied, r_turned = count("r_copied", 1), count("r_turned", 1)
        r_mm, r_z, r_exp, r_step = count("r_mm", 1), count("r_z", 1), count("r_exp", 1), count("r_step", 8)
        gu_done, (tanh_done, hg_done, hid_done) = count("gu_done", 4 * EC), (count(n, 2 * EC) for n in ("tanh_done", "hg_done", "hid_done"))
        down_done, comb_done, out_stored = count("down_done", E * T), count("comb_done", E * T), count("out_stored", 16 * (1 + NB))

        parts_d = nc.dram_tensor("parts_scratch", (2, 3, D, COLS), BF16).ap()
        nm_d = nc.dram_tensor("neg_max_scratch", (2, NB, HEADS, S), BF16).ap()
        qtab_d = nc.dram_tensor("qtab_scratch", (3, NORD, HEADS, NB, PAD), BF16).ap()

        QK_BANK = [7, 6]
        GU_BANKS = [(0, 1), (3, 4), (2, 5)]
        V_BANK = [6, 4, 6, 3]
        CTX_BANK = [6, 6, 6, 6, 7]
        X2_BANK = [7, 7, 7, 7, 6]
        X1_BANK = [6, 7, 6, 7, 6]
        PV_BANK = [5, 2]

        def between(j):
            return {0: [("ctx", 4)], 1: [("norm1", 2)], 2: [("x1", 0), ("norm1", 3)], 3: [("x1", 1), ("norm1", 4)],
                    4: [("x1", 2), ("norm2", 3)], 5: [("x1", 3), ("norm2", 4)], 6: [("x1", 4)], 7: [("x2", 3)], 8: [("x2", 4)],
                    9: [("qk", 0), ("qk", 1)], 10: [("qk", 2), ("qk", 3)], 11: [("qk", 4), ("qk", 5)],
                    13: [("router", 0)], 15: [("logits", 0), ("gates", 0)], 16: [("gates", 1)], 17: [("gates", 2)],
                    18: [("gates", 3)], 19: [("gates", 4)], 20: [("gates", 5)]}.get(j, [])

        NORMED_EARLY = 2
        def among(s):
            return {0: [("quant", 1)], 1: [("quant", 2)], 2: [("stat", 0), ("stat", 1)], 3: [("stat", 2), ("stat", 3)],
                    4: [("ctx", 0)], 5: [("stat", 4)], 6: [("norm2", 0)] + [("mv", t) for t in range(T)],
                    7: [("x2", 0), ("ctx", 1)], 8: [("norm1", 0)],
                    9: [("norm2", 1), ("norm1", 1)], 10: [("ctx", 2)], 11: [("x2", 1)],
                    12: [("norm2", 2), ("unit", E * T - 2), ("x2", 2), ("unit", E * T - 1), ("ctx", 3)]}.get(s, [])

        FIRST = 2 * T
        WITH_VALUES = FIRST + 4
        SLOT = [1, 3, 5, 9]

        def unit(u, tail=False):
            v = u % FIRST
            if u < FIRST:
                bank = 6 + v % 2
            elif tail:
                bank = 2 + v % 2
            else:
                bank = 2 if u < WITH_VALUES - 1 else 7 if u < WITH_VALUES + len(SLOT) else 5 if u == E * T - 2 else 2
            return v // 2, v % 2 + 2 * (u // FIRST), bank

        def unit_after(s):
            return [WITH_VALUES + i for i in range(len(SLOT)) if SLOT[i] == s]

        out_g = a["out"].rearrange("(g b) s d -> g b s d", b=NB)

        def qk_source(i):
            if i % 2 == 0:
                return ps[:, QK_BANK[i % 2], 0:NB * TXT].rearrange("p (b c) -> p b c", b=NB)
            return ps[:, QK_BANK[i % 2], 0:NB * 32].rearrange("p (b c) -> p b c", b=NB)[:, :, 0:IMG]

        def qk_part(i, k):
            c = slice(0, TXT) if i % 2 == 0 else slice(TXT, S)
            return qk_parts[:, i // 2, k].rearrange("p (b c) -> p b c", b=NB)[:, :, c]

        def qk_rest_of(i):
            return qk_rest_txt[:] if i % 2 == 0 else qk_rest_img[:]

        def pass_waits(eng):
            eng.sem_inc(passed, 1)

        block = ctx.enter_context(nc.Block())

        @block.sync
        def _(sp):
            def load_tokens(n):
                emb_in.wait(sp, n - 1)
                pass_waits(sp)
                conv_done.wait(sp, n - 1)
                pass_waits(sp)
                sp.dma_start(token_ids[:], a["ids"][n]).then_inc(ids_in.handle, 16)
                sp.dma_start(patches[:], a["patches"][n]).then_inc(patches_in.handle, 16)

            SHARES = [(0, 0, P, 0, 0), (1, 0, D - P, 0, P), (1, D - P, P, 1, 0), (2, 0, P, 1, 2 * P - D)]

            def load_product(stack, qk, i, parts):
                sp.dma_start(stack[HD * i:HD * (i + len(parts))].rearrange("r h c -> r (h c)"),
                             parts_d[qk, parts[0]:parts[-1] + 1].rearrange("s (d h) c -> (s d) (h c)", d=HD)
                             ).then_inc(stacks_in.handle, 16)

            def exchange(n):
                stacks_in.wait(sp, n, 0)
                pass_waits(sp)
                for t, r0, r1, qk, f in SHARES:
                    qk_low.wait(sp, n, 2 * t + 2)
                    qk_mid.wait(sp, n, 2 * t + 2)
                    sp.dma_start(parts_d[qk, :, f:f + r1 - r0, :].rearrange("s r c -> r s c"),
                                 qk_parts[r0:r1, t]).then_inc(parts_stored.handle, 16)
                s2_done.wait(sp, n, 0)
                pass_waits(sp)
                parts_stored.wait(sp, n)
                load_product(q_stack, 0, 0, [0, 1])
                load_product(q_stack, 0, 2, [0, 1])
                load_product(q_stack, 0, 4, [2])
                load_product(q_stack, 0, 5, [0])
                load_product(k_stack, 1, 0, [0, 1])
                load_product(k_stack, 1, 2, [1])
                load_product(k_stack, 1, 3, [0])
                load_product(k_stack, 1, 4, [0])
                load_product(k_stack, 1, 5, [2])

            def load_neg_max(n):
                nm_high.wait(sp, n)
                nm_done.wait(sp, n)
                nb = NB * HEADS
                sp.dma_start(nm_d[:, :, :, 0:TXT].rearrange("i b h c -> (b h) i c"), neg_max[0:nb]
                             ).then_inc(nm_stored.handle, 16)
                for i in range(2):
                    sp.dma_start(nm_d[i, :, :, TXT:S].rearrange("b (t q) c -> (b t) q c", q=4),
                                 neg_max[nb:NM, i].rearrange("t (q s) -> t q s", q=4)[:, :, 0:IMG]
                                 ).then_inc(nm_stored.handle, 16)
                nm_stored.wait(sp, n)
                for b in range(NB):
                    sp.dma_start(q_stack[MAX0:P, :, PAD * b:PAD * b + S], nm_d[:, b]).then_inc(nm_in[b].handle, 16)

            def store_out(n):
                comb_done.wait(sp, n, FIRST + 2 * NB)
                pass_waits(sp)
                sp.dma_start(out_g[n, :, IMG:S, :].rearrange("b s d -> s b d"), h2[:, 0:NB, :]
                             ).then_inc(out_stored.handle, 16)
                comb_done.wait(sp, n)
                pass_waits(sp)
                for b in range(NB):
                    sp.dma_start(out_g[n, b, 0:IMG, :], h2[32 * b:32 * b + IMG, NB, :]
                                 ).then_inc(out_stored.handle, 16)

            sp.dma_start(token_ids[:], a["ids"][0]).then_inc(ids_in.handle, 16)
            sp.dma_start(alpha_t, a["alpha_t"]).then_inc(tab_loaded, 16)
            sp.dma_start(cheb, a["cheb"]).then_inc(tab_loaded, 16)
            sp.dma_start(patches[:], a["patches"][0]).then_inc(patches_in.handle, 16)
            sp.dma_start(w_conv[:], a["w_conv"]).then_inc(small_loaded, 16)
            sp.dma_start(pos_in, a["pos"]).then_inc(small_loaded, 16)
            sp.dma_start(pos_bias[:], a["conv_b"]).then_inc(small_loaded, 16)
            sp.dma_start(ident[:], a["ident"]).then_inc(small_loaded, 16)
            sp.dma_start(qk_bias[:], a["bqk"]).then_inc(small_loaded, 16)
            for i in range(4):
                sp.dma_start(w_stage[i], a["w_split"][i]).then_inc(w_loaded[i], 16)
            sp.wait_ge(tab_ready, 1)
            for b in range(NB):
                sp.dma_start(qtab_d[:, :, :, b].rearrange("i n h c -> h (i n) c"), q_tab).then_inc(tab_stored, 16)
            sp.dma_start(k_stack[BIAS0:P].rearrange("r h c -> r (h c)"), a["k_tail"]).then_inc(k_tail_in, 16)
            sp.wait_ge(tab_stored, 16 * NB)
            n1, n2 = BIAS0 + 3 * NORD, NORD - 2
            sp.dma_start(q_stack[BIAS0:n1].rearrange("r h c -> r (h c)"),
                         qtab_d.rearrange("i n h b c -> (i n) (h b c)")).then_inc(tables_in, 16)
            for i in range(3):
                sp.dma_start(q_stack[n1 + n2 * i:n1 + n2 * (i + 1)].rearrange("r h c -> r (h c)"),
                             qtab_d[BIAS_Q2[i], 2:NORD].rearrange("n h b c -> n (h b c)")).then_inc(tables_in, 16)
            sp.dma_start(v_bias[:], a["bv"]).then_inc(late_loaded, 16)
            sp.dma_start(r_bias[:], a["r_bias"]).then_inc(late_loaded, 16)
            sp.dma_start(pick[:], a["pick"]).then_inc(late_loaded, 16)
            exchange(0)
            for i in range(4, 8):
                sp.wait_ge(w_split, i - 3)
                sp.dma_start(w_stage[i % 4], a["w_split"][i]).then_inc(w_loaded[i % 4], 16)
            sp.dma_start(w_down[:], a["w_down"]).then_inc(down_loaded, 16)

            def group(g, first=False, left=2):
                load_neg_max(g)
                if left > 1:
                    load_tokens(g + 2)
                if not first:
                    store_out(g - 1)
                if left:
                    exchange(g + 1)

            load_tokens(1)
            group(0, first=True)
            with sp.Fori(1, G - 2) as g:
                group(g)
            group(G - 2, left=1)
            group(G - 1, left=0)
            store_out(G - 1)
            out_stored.wait(sp, G - 1)

        @block.gpsimd
        def _(pool):
            nc.gpsimd.memset(eps[:], EPS)
            nc.gpsimd.memset(minus_half[:], -0.5).then_inc(eps_ready, 1)
            pool.wait_ge(eps_ready, 1)

            def gather(n):
                ids_in.wait(pool, n)
                if not (isinstance(n, int) and n == 0):
                    tok_kept.wait(pool, n - 1)
                    pass_waits(pool)
                    xn1_done.wait(pool, n - 1)
                pass_waits(pool)
                for b in range(NB):
                    nc.gpsimd.indirect_dma_start(
                        out=tok[:, b, :], out_offset=None, in_=a["table"],
                        in_offset=bass.IndirectOffsetOnAxis(ap=token_ids[:, b:b + 1], axis=0),
                    ).then_inc(emb_in.handle, 16)

            def add_v_bias(n):
                tok_kept.wait(pool, n)
                nc.gpsimd.tensor_tensor(h1[:], h1[:], v_bias[:].unsqueeze(1).broadcast_to([P, T, D]), ALU.add
                                        ).then_inc(v_biased.handle, 1)

            def inv_std(n, k, t0, t1):
                ln_mv[k].wait(pool, n, t1)
                nc.gpsimd.tensor_tensor(var_eps[:, k, t0:t1], mv[:, k, t0:t1, 1], eps[:, t0:t1], ALU.add
                                        ).then_inc(ln_eps[k].handle, t1 - t0)
                ln_eps[k].wait(pool, n, t1)
                nc.gpsimd.tensor_tensor(rstd[:, k, t0:t1], var_eps[:, k, t0:t1], minus_half[:, t0:t1], ALU.pow
                                        ).then_inc(rstd_ready[k].handle, t1 - t0)

            def low_parts(n):
                for i in range(2 * QKC):
                    qk_mid.wait(pool, n, i + 1)
                    nc.gpsimd.tensor_tensor(qk_part(i, 2), qk_rest_of(i), qk_part(i, 1), ALU.subtract
                                            ).then_inc(qk_low.handle, 1)

            gather(0)
            inv_std(0, 0, 0, T)
            low_parts(0)
            pool.wait_ge(late_loaded, 16 * 3)

            def group(g, left=1):
                if left:
                    gather(g + 1)
                add_v_bias(g)
                inv_std(g, 1, 0, 1)
                if left:
                    inv_std(g + 1, 0, 0, T)
                inv_std(g, 1, 1, 2)
                inv_std(g, 1, 2, 3)
                inv_std(g, 1, 3, T)
                if left:
                    low_parts(g + 1)

            group(0)
            with pool.Fori(1, G - 1) as g:
                group(g)
            group(G - 1, left=0)

        @block.scalar
        def _(act):
            def high_x(n, t, done, high, xt, bank):
                done.wait(act, n, t + 1)
                nc.scalar.activation(xt[:, 0:2, P * t:P * (t + 1)],
                                     ps[:, bank, 0:2 * P].rearrange("p (k c) -> p k c", k=2), ACT.Copy
                                     ).then_inc(high.handle, 1)

            def twice(n, t):
                xn1_normed.wait(act, n, t + 1)
                nc.scalar.activation(xn[0][:, t, D:2 * P], xn[0][:, t, P:D], ACT.Copy).then_inc(xn1_done.handle, 1)

            def keep_tokens(n):
                if not (isinstance(n, int) and n == 0):
                    comb_done.wait(act, n - 1, FIRST - 1)
                quant.wait(act, n)
                img_tokens.wait(act, n)
                nc.scalar.activation(h1[:], tok[:], ACT.Copy).then_inc(tok_kept.handle, 1)

            def high_qk(n, i):
                if i == 0:
                    parts_stored.wait(act, n, 0)
                qk_done.wait(act, n, i + 1)
                nc.scalar.activation(qk_part(i, 0), qk_source(i), ACT.Identity, bias=qk_bias[:, i // 2:i // 2 + 1]
                                     ).then_inc(qk_high.handle, 1)

            def exps(g, s):
                bank = 3 * (s % 2)
                s2_done.wait(act, g, s + 1)
                if s >= 2:
                    pv_done.wait(act, g, s - 1)
                nc.scalar.activation(prob_t[s % 2].rearrange("p (k h) c -> p k (h c)", k=2),
                                     ps[:, bank:bank + 2, 0:2 * S], ACT.Exp, scale=0.25)
                nc.scalar.activation(prob_i[s % 2], ps[:, bank, 2 * S:3 * S], ACT.Exp, scale=0.25
                                     ).then_inc(exp_done.handle, 1)

            def copy_logits(g):
                r_mm.wait(act, g)
                nc.scalar.activation(logits[:, 0:NB * TXT], ps[0:4, 6, 0:NB * TXT], ACT.Copy)
                nc.scalar.activation(logits[:, NB * TXT:T * P], ps[0:4, 7, 0:P], ACT.Copy).then_inc(r_copied.handle, 1)

            def router_exp(g):
                r_z.wait(act, g)
                nc.scalar.activation(rt[:, 1], rt[:, 0], ACT.Exp, scale=-1.0).then_inc(r_exp.handle, 1)

            def tanh(g, j):
                gu_done.wait(act, g, 2 * j + 1)
                if j >= 2:
                    hg_done.wait(act, g, j - 1)
                nc.scalar.activation(th[:, j % 2], ps[:, GU_BANKS[j % 3][0], 0:HALF], ACT.Tanh, scale=0.5
                                     ).then_inc(tanh_done.handle, 1)

            def neg_high(g):
                mt_done.wait(act, g)
                nc.scalar.activation(neg_max[:, 0], ps[0:NM, 5, 0:P], ACT.Copy, scale=-1.0
                                     ).then_inc(nm_high.handle, 1)

            def high_weights(i):
                act.wait_ge(w_loaded[i % 4], 16 * (i // 4 + 1))
                nc.scalar.activation(w_hi[:, :, WPIECE * i:WPIECE * (i + 1)], w_stage[i % 4], ACT.Copy
                                     ).then_inc(w_high, 1)

            for i in range(4):
                high_weights(i)
            for t in range(T):
                twice(0, t)
            for t in range(T):
                high_x(0, t, x1t_done, x1_high, x1t, X1_BANK[t])
            act.wait_ge(small_loaded, 16 * 5)
            act.wait_ge(consts_ready, 1)
            for i in range(2 * QKC):
                high_qk(0, i)
            for i in range(4, 8):
                high_weights(i)

            def values(g, batches):
                for b in batches:
                    v_mm.wait(act, g, b + 2)
                    nc.scalar.activation(v_txt[:, b, :, 0:HD], ps[:, V_BANK[b], 0:D].rearrange("p (h d) -> p h d", d=HD), ACT.Copy
                                         ).then_inc(v_txt_done.handle, 1)

            def img_values(g):
                added.wait(act, g, 0)
                v_mm.wait(act, g, 1)
                nc.scalar.activation(v_all, ps[:, 7, 0:D], ACT.Copy).then_inc(v_all_done.handle, 1)

            def group(g, first=False, left=1):
                keep_tokens(g)
                img_values(g)
                values(g, [0, 1])
                neg_high(g)
                values(g, [2, 3])
                if first:
                    act.wait_ge(w_split, 8)
                for s in range(NB * QUADS + 1):
                    if s < NB * QUADS:
                        exps(g, s)
                    for what, t in among(s):
                        if what == "x2":
                            high_x(g, t, x2t_done, x2_high, x2t, X2_BANK[t])
                if left:
                    for t in range(NORMED_EARLY):
                        twice(g + 1, t)
                for j in range(2 * EC):
                    tanh(g, j)
                    for what, i in between(j - 1):
                        if what == "norm1" and left:
                            twice(g + 1, i)
                    for what, i in between(j):
                        if what == "x2":
                            high_x(g, i, x2t_done, x2_high, x2t, X2_BANK[i])
                        if what == "router":
                            copy_logits(g)
                        if what == "logits":
                            router_exp(g)
                        if what == "x1" and left:
                            high_x(g + 1, i, x1t_done, x1_high, x1t, X1_BANK[i])
                        if what == "qk" and left:
                            high_qk(g + 1, i)

            group(0, first=True)
            with act.Fori(1, G - 1) as g:
                group(g)
            group(G - 1, left=0)

        @block.vector
        def _(dve):
            v = nc.vector

            def quantise(n, step):
                e = tok[:, 0:NB]
                if step == 0:
                    emb_in.wait(dve, n)
                    v.tensor_scalar(e, e, LEVELS, QMIN, ALU.mult, ALU.max).then_inc(q_a.handle, 1)
                if step == 1:
                    q_a.wait(dve, n)
                    v.tensor_scalar(e, e, QMAX, ROUND, ALU.min, ALU.add).then_inc(q_b.handle, 1)
                if step == 2:
                    q_b.wait(dve, n)
                    v.tensor_scalar(e, e, ROUND, 1.0 / LEVELS, ALU.subtract, ALU.mult).then_inc(quant.handle, 1)
                if step == 3:
                    conv_done.wait(dve, n)
                    if not (isinstance(n, int) and n == 0):
                        tok_kept.wait(dve, n - 1)
                    v.tensor_tensor(tok[:, NB], ps[:, 4, 0:D], pos_bias[:], ALU.add).then_inc(img_tokens.handle, 1)

            def stat(n, k, t, src):
                v.bn_stats(stats[:, k, t], src[:, t]).then_inc(ln_stat[k].handle, 1)

            def mean_var(n, k, t):
                ln_stat[k].wait(dve, n, t + 1)
                pass_waits(dve)
                v.bn_aggr(mv[:, k, t], stats[:, k, t]).then_inc(ln_mv[k].handle, 1)

            def norm(n, k, t, src, done):
                rstd_ready[k].wait(dve, n, t + 1)
                if not (isinstance(n, int) and n == 0):
                    (x2t_done if k else x1t_done).wait(dve, n - 1, t + 1)
                m, r = mv[:, k, t, 0:1], rstd[:, k, t:t + 1]
                ins = v.tensor_scalar(xn[k][:, t, 0:D], src[:, t], m, r, ALU.subtract, ALU.mult)
                if k:
                    ins = v.tensor_scalar(xn[k][:, t, D:2 * P], src[:, t, P:D], m, r, ALU.subtract, ALU.mult)
                ins.then_inc(done.handle, 1)

            def split_x(n, t, high, split, xt, bank):
                high.wait(dve, n, t + 1)
                src, c = ps[:, bank, 0:2 * P], slice(P * t, P * (t + 1))
                v.tensor_tensor(xt[:, 2, c], src[:, 0:P], xt[:, 0, c].bitcast(F32), ALU.subtract)
                v.tensor_tensor(xt[64:P, 1, c], src[64:P, P:2 * P], xt[64:P, 1, c].bitcast(F32), ALU.subtract
                                ).then_inc(split.handle, 1)

            def split_qk(n, i):
                qk_high.wait(dve, n, i + 1)
                if i >= 2:
                    qk_low.wait(dve, n, i - 1)
                v.scalar_tensor_tensor(qk_rest_of(i), qk_source(i), qk_bias[:, i // 2:i // 2 + 1], qk_part(i, 0),
                                       ALU.add, ALU.subtract).then_inc(qk_sub.handle, 1)
                qk_sub.wait(dve, n, i + 1)
                v.tensor_copy(qk_part(i, 1), qk_rest_of(i)).then_inc(qk_mid.handle, 1)

            def values(g):
                v_img_mm.wait(dve, g)
                v.tensor_copy(v_img[:, :, :, 0:HD], ps[:, 7, 0:D].rearrange("p (b t d) -> p b t d", b=NB, d=HD)
                              ).then_inc(v_img_done.handle, 1)

            def maxima(g, s):
                b, t, bank = s // QUADS, s % QUADS, 2 * (s % 2)
                s1_done.wait(dve, g, s + 1)
                c = HEADS * b + 4 * t
                v.tensor_reduce(mx[:, c:c + 4].rearrange("p (k h) -> p k h", k=2),
                                ps[:, bank:bank + 2, 0:2 * S].rearrange("p k (h c) -> p k h c", h=2), AX, ALU.max)
                c = NB * HEADS + QUADS * b + t
                v.tensor_reduce(mx[:, c:c + 1], ps[:, bank, 2 * S:3 * S], AX, ALU.max).then_inc(max_done.handle, 1)

            def neg_low(g):
                nm_high.wait(dve, g)
                v.scalar_tensor_tensor(neg_max[:, 1], ps[0:NM, 5, 0:P], -1.0, neg_max[:, 0],
                                       ALU.mult, ALU.subtract).then_inc(nm_done.handle, 1)

            def copy_ctx(g, s):
                b, t, bank = s // QUADS, s % QUADS, PV_BANK[s % 2]
                pv_done.wait(dve, g, s + 1)
                v.tensor_copy(ctxt[:, b, t], ps[:, bank, 0:TXT])
                v.tensor_copy(ctxi[:, t, 32 * b:32 * b + IMG], ps[:, bank, TXT:S]).then_inc(pv_copied.handle, 1)

            def add_ctx(g, t):
                c = ps[:, CTX_BANK[t], 0:HEADS * 32].rearrange("p (h d) -> p h d", d=32)
                ct_done.wait(dve, g, t + 1)
                v.reciprocal(rsum[:], c[:, :, HD]).then_inc(ct_recip.handle, 1)
                ct_recip.wait(dve, g, t + 1)
                v.tensor_tensor(ctx_n[:].rearrange("p (h d) -> p h d", d=HD), c[:, :, 0:HD],
                                rsum[:].unsqueeze(2).broadcast_to([P, HEADS, HD]), ALU.mult
                                ).then_inc(ct_norm.handle, 1)
                ct_norm.wait(dve, g, t + 1)
                if t == 0:
                    v_biased.wait(dve, g)
                v.tensor_tensor(h1[:, t], ctx_n[:], h1[:, t], ALU.add).then_inc(added.handle, 1)
                added.wait(dve, g, t + 1)
                stat(g, 1, t, h1)
                mean_var(g, 1, t)

            def gates(g, k):
                z, e, p, keep, w, tmp = rt[:, 0], rt[:, 1], rt[:, 2], rt[:, 3], rt[:, 4], rt[:, 5]
                if k == 0:
                    r_turned.wait(dve, g)
                    v.tensor_tensor(z, ps[:, 6, 0:4 * T].rearrange("p (t e) -> p t e", e=4)[:, :, 0:3], r_bias[:], ALU.add
                                    ).then_inc(r_z.handle, 1)
                if k == 1:
                    r_exp.wait(dve, g)
                    v.tensor_scalar(e, e, 1.0, None, ALU.add).then_inc(r_step.handle, 1)
                    r_step.wait(dve, g, 1)
                    v.reciprocal(p, e).then_inc(r_step.handle, 1)
                if k == 2:
                    r_step.wait(dve, g, 2)
                    v.tensor_tensor(tmp[:, :, 0], p[:, :, 0], p[:, :, 1], ALU.is_ge)
                    v.tensor_tensor(tmp[:, :, 1], p[:, :, 0], p[:, :, 2], ALU.is_ge)
                    v.tensor_tensor(tmp[:, :, 2], p[:, :, 1], p[:, :, 2], ALU.is_ge).then_inc(r_step.handle, 1)
                if k == 3:
                    r_step.wait(dve, g, 3)
                    v.tensor_tensor(keep[:, :, 0], tmp[:, :, 0], tmp[:, :, 1], ALU.max)
                    v.tensor_tensor(keep[:, :, 2], tmp[:, :, 1], tmp[:, :, 2], ALU.min)
                    v.tensor_scalar(rt[:, 6, :, 0], tmp[:, :, 0], -1.0, 1.0, ALU.mult, ALU.add).then_inc(r_step.handle, 1)
                    r_step.wait(dve, g, 4)
                    v.tensor_tensor(keep[:, :, 1], rt[:, 6, :, 0], tmp[:, :, 2], ALU.max)
                    v.tensor_scalar(keep[:, :, 2], keep[:, :, 2], -1.0, 1.0, ALU.mult, ALU.add).then_inc(r_step.handle, 1)
                if k == 4:
                    r_step.wait(dve, g, 5)
                    v.tensor_tensor(w, keep, p, ALU.mult).then_inc(r_step.handle, 1)
                    r_step.wait(dve, g, 6)
                    v.tensor_reduce(rt[:, 6, :, 1], w, AX, ALU.add).then_inc(r_step.handle, 1)
                if k == 5:
                    r_step.wait(dve, g, 7)
                    v.reciprocal(rt[:, 6, :, 2], rt[:, 6, :, 1]).then_inc(r_step.handle, 1)
                    r_step.wait(dve, g, 8)
                    v.scalar_tensor_tensor(rt[:, 7], w, 0.5, rt[:, 6, :, 2].unsqueeze(2).broadcast_to([P, T, 3]),
                                           ALU.mult, ALU.mult)

            def hidden(g, j):
                hf, ec = j // EC, j % EC
                bg, bu = GU_BANKS[j % 3]
                tanh_done.wait(dve, g, j + 1)
                v.scalar_tensor_tensor(hg[:, j % 2], th[:, j % 2], 1.0, ps[:, bg, 0:HALF], ALU.add, ALU.mult
                                       ).then_inc(hg_done.handle, 1)
                hg_done.wait(dve, g, j + 1)
                gu_done.wait(dve, g, 2 * j + 2)
                v.tensor_tensor(hid[:, ec, HALF * hf:HALF * (hf + 1)], hg[:, j % 2], ps[:, bu, 0:HALF], ALU.mult
                                ).then_inc(hid_done.handle, 1)

            def combine(n, u, tail=False):
                t, e, bank = unit(u, tail)
                if u == 0:
                    out_stored.wait(dve, n, 0)
                down_done.wait(dve, n, u + 1)
                if e:
                    comb_done.wait(dve, n, u)
                v.scalar_tensor_tensor(h2[:, t], ps[:, bank, 0:D], rt[:, 7, t, e - 1:e] if e else 0.5,
                                       h2[:, t] if e else h1[:, t], ALU.mult, ALU.add).then_inc(comb_done.handle, 1)

            def low_weights(i):
                dve.wait_ge(w_high, i + 1)
                c = slice(WPIECE * i, WPIECE * (i + 1))
                v.tensor_tensor(w_lo[:, :, c], w_stage[i % 4], w_hi[:, :, c].bitcast(F32), ALU.subtract
                                ).then_inc(w_split, 1)

            v.memset(q_tab[:, :, S:PAD], 0.0)
            v.memset(q_stack[BIAS0:P].rearrange("p h (b c) -> p (h b) c", c=PAD)[:, :, S:PAD], 0.0)
            v.memset(qk_parts[:].rearrange("p t s (b c) -> p (t s b) c", c=PAD)[:, :, S:PAD], 0.0)
            dve.wait_ge(tab_mm, 1)
            tab = ps[0:HEADS, 6:8, 0:NORD * S // 2].rearrange("h k (n c) -> h k n c", c=S)
            part = [q_tab[:, NORD * i:NORD * (i + 1), 0:S].rearrange("h (k n) c -> h k n c", k=2) for i in range(3)]
            rest = q_tab_rest.rearrange("h (k n c) -> h k n c", k=2, c=S)
            v.tensor_copy(part[0], tab).then_inc(tab_part, 1)
            dve.wait_ge(tab_part, 1)
            v.tensor_tensor(rest, tab, part[0], ALU.subtract).then_inc(tab_part, 1)
            dve.wait_ge(tab_part, 2)
            v.tensor_copy(part[1], rest).then_inc(tab_part, 1)
            dve.wait_ge(tab_part, 3)
            v.tensor_tensor(part[2], rest, part[1], ALU.subtract).then_inc(tab_ready, 1)
            dve.wait_ge(small_loaded, 16 * 5)
            v.tensor_tensor(pos_bias[:], pos_bias[:], pos_in, ALU.add).then_inc(pos_ready, 1)
            dve.wait_ge(pos_ready, 1)
            for k in range(4):
                quantise(0, k)
            quant.wait(dve, 0)
            img_tokens.wait(dve, 0)
            for t in range(T):
                stat(0, 0, t, tok)
            for t in range(T):
                mean_var(0, 0, t)
            v.memset(mx[:], 0.0)
            v.memset(v_txt[:, :, :, HD:32], 0.0)
            v.memset(v_img[:, :, :, HD:32], 0.0)
            v.memset(ctxi[:], 1.0).then_inc(clear_done, 1)
            dve.wait_ge(clear_done, 1)
            v.memset(v_txt[:, :, :, HD:HD + 1], 1.0)
            for q in range(4):
                rows = slice(32 * q, 32 * q + IMG)
                ins = v.memset(v_img[rows, :, :, HD:HD + 1], 1.0)
            ins.then_inc(consts_ready, 1)
            dve.wait_ge(consts_ready, 1)
            low_weights(0)
            for t in range(T):
                norm(0, 0, t, tok, xn1_normed)
            for t in range(T):
                split_x(0, t, x1_high, x1_split, x1t, X1_BANK[t])
            for i in range(2 * QKC):
                split_qk(0, i)
                if i % 2:
                    low_weights(1 + i // 2)

            dve.wait_ge(late_loaded, 16 * 3)

            def group(g, first=False, left=1):
                if not first:
                    combine(g - 1, 0)
                for s in range(NB * QUADS):
                    if not first and 0 < s < FIRST:
                        combine(g - 1, s)
                    maxima(g, s)
                neg_low(g)
                values(g)
                if first:
                    for i in range(4, 8):
                        low_weights(i)
                for i in range(4):
                    if left and i == 2:
                        quantise(g + 1, 3)
                    if not first:
                        combine(g - 1, FIRST + i)
                if left:
                    quantise(g + 1, 0)

                def event(what, i):
                    if what == "ctx":
                        add_ctx(g, i)
                    if what == "norm2":
                        norm(g, 1, i, h1, xn2_done)
                    if what == "x2":
                        split_x(g, i, x2_high, x2_split, x2t, X2_BANK[i])
                    if what == "gates":
                        gates(g, i)
                    if what == "unit" and not first:
                        combine(g - 1, i)
                    if left:
                        if what == "quant":
                            quantise(g + 1, i)
                        if what == "stat":
                            if i == 0:
                                quant.wait(dve, g + 1)
                                img_tokens.wait(dve, g + 1)
                            stat(g + 1, 0, i, tok)
                        if what == "mv":
                            mean_var(g + 1, 0, i)
                        if what == "norm1":
                            norm(g + 1, 0, i, tok, xn1_normed)
                        if what == "x1":
                            split_x(g + 1, i, x1_high, x1_split, x1t, X1_BANK[i])
                        if what == "qk":
                            split_qk(g + 1, i)

                for s in range(NB * QUADS + 1):
                    if not first:
                        for u in unit_after(s):
                            combine(g - 1, u)
                    if s:
                        copy_ctx(g, s - 1)
                    for what, i in among(s):
                        event(what, i)
                for j in range(2 * EC):
                    hidden(g, j)
                    for what, i in between(j):
                        event(what, i)

            group(0, first=True)
            with dve.Fori(1, G - 1) as g:
                group(g)
            group(G - 1, left=0)
            for u in range(E * T):
                combine(G - 1, u, tail=True)

        @block.tensor
        def _(pe):
            mm = nc.tensor.matmul

            def split_mm(out, w, x, lhs_is_x):
                passes = ((w_hi, 0, 0), (w_hi, 0, 2), (w_lo, 0, 0), (w_hi, 1, 1), (w_lo, 1, 1))
                for i, (wt, wk, xk) in enumerate(passes):
                    l, r = wt[:, wk, w], x(xk)
                    if lhs_is_x:
                        l, r = r, l
                    ins = mm(out, l, r, start=(i == 0), stop=(i == 4))
                return ins

            def conv(n):
                patches_in.wait(pe, n)
                for c in range(KCONV):
                    ins = mm(ps[:, 4, 0:D], patches[:, c], w_conv[:, c], start=(c == 0), stop=(c == KCONV - 1))
                ins.then_inc(conv_done.handle, 1)

            def turn(n, t, x, xn_done, done, bank):
                xn_done.wait(pe, n, t + 1)
                nc.tensor.transpose(ps[:, bank, 0:P], x[:, t, 0:P], ident[:])
                nc.tensor.transpose(ps[:, bank, P:2 * P], x[:, t, P:2 * P], ident[:]).then_inc(done.handle, 1)

            def turn_x1(n, t):
                if t >= 2:
                    x1_split.wait(pe, n, t - 1)
                turn(n, t, xn[0], xn1_done, x1t_done, X1_BANK[t])

            def qk(n, i):
                c = slice(0, NB * TXT) if i % 2 == 0 else slice(NB * TXT, T * P)
                at = C_QK + P * (i // 2)
                if i >= 2:
                    qk_sub.wait(pe, n, i - 1)
                split_mm(ps[:, QK_BANK[i % 2], 0:c.stop - c.start], slice(at, at + P),
                         lambda k: x1t[:, k, c], False).then_inc(qk_done.handle, 1)

            def values_all(g):
                img = slice(NB * TXT, T * P)
                split_mm(ps[:, 7, 0:D], slice(C_V, C_V + D), lambda k: x1t[:, k, img], True).then_inc(v_mm.handle, 1)

            def values(g, b):
                if b == 2:
                    v_txt_done.wait(pe, g, 1)
                split_mm(ps[:, V_BANK[b], 0:D], slice(C_V, C_V + D), lambda k: x1t[:, k, P * b:P * (b + 1)], True
                         ).then_inc(v_mm.handle, 1)

            def pick_img_values(g):
                v_all_done.wait(pe, g)
                for i in range(4):
                    for b in range(NB):
                        c = QUADS * HD * b
                        ins = mm(ps[32 * i:32 * i + 32, 7, c:c + QUADS * HD].rearrange("p (t d) -> p t d", d=HD),
                                 pick[:, b], v_all.rearrange("p (t q d) -> p q t d", q=4, d=HD)[:, i],
                                 start=True, stop=True)
                ins.then_inc(v_img_mm.handle, 1)

            def scores(left, right, rows, b, t, bank, done):
                c = PAD * b
                for i in range(4):
                    mm(ps[:, bank + i // 2, S * (i % 2):S * (i % 2 + 1)], left[rows, 4 * t + i, c:c + TXT],
                       right[rows, 4 * t + i, c:c + S], start=True, stop=True)
                for i in range(4):
                    ins = mm(ps[32 * i:32 * i + 32, bank, 2 * S:3 * S], left[rows, 4 * t + i, c + TXT:c + PAD],
                             right[rows, 4 * t + i, c:c + S], start=True, stop=True)
                ins.then_inc(done.handle, 1)

            def scores_by_query(g, s):
                if s >= 2:
                    max_done.wait(pe, g, s - 1)
                scores(q_stack, k_stack, slice(0, MAX0), s // QUADS, s % QUADS, 2 * (s % 2), s1_done)

            def scores_by_key(g, s):
                if s % QUADS == 0:
                    nm_in[s // QUADS].wait(pe, g)
                if s >= 2:
                    exp_done.wait(pe, g, s - 1)
                scores(k_stack, q_stack, slice(0, P), s // QUADS, s % QUADS, 3 * (s % 2), s2_done)

            def context(g, s):
                b, t = s // QUADS, s % QUADS
                exp_done.wait(pe, g, s + 1)
                bank = PV_BANK[s % 2]
                if s >= 2:
                    pv_copied.wait(pe, g, s - 1)
                for i in range(4):
                    mm(ps[32 * i:32 * i + 32, bank, 0:S], v_txt[:, b, 4 * t + i], prob_t[s % 2][:, i],
                       start=True, stop=False)
                for i in range(4):
                    q = slice(32 * i, 32 * i + 32)
                    ins = mm(ps[q, bank, 0:S], v_img[q, b, t], prob_i[s % 2][q], start=False, stop=True)
                ins.then_inc(pv_done.handle, 1)

            def turn_ctx(g, t):
                pv_copied.wait(pe, g, QUADS * min(t + 1, NB))
                if t == NB:
                    x2_split.wait(pe, g, 3)
                elif t:
                    added.wait(pe, g, t)
                for k in range(QUADS):
                    src = ctxt[:, t, k] if t < NB else ctxi[:, k]
                    ins = nc.tensor.transpose(ps[:, CTX_BANK[t], P * k:P * (k + 1)], src, ident[:])
                ins.then_inc(ct_done.handle, 1)

            def turn_x2(g, t, first, left):
                if 0 < t < 3:
                    x2_split.wait(pe, g, t)
                if t < 3 and not first:
                    comb_done.wait(pe, g - 1, WITH_VALUES + len([s for s in SLOT if s < [7, 11, 12][t]]))
                if t >= 3 and left:
                    x1_split.wait(pe, g + 1, t + 1)
                turn(g, t, xn[1], xn2_done, x2t_done, X2_BANK[t])

            def router(g, left):
                x2_split.wait(pe, g)
                if left:
                    qk_sub.wait(pe, g + 1)
                for bank, c in ((6, slice(0, NB * TXT)), (7, slice(NB * TXT, T * P))):
                    ins = split_mm(ps[0:4, bank, 0:c.stop - c.start], slice(C_R, C_R + 4), lambda k: x2t[:, k, c], False)
                ins.then_inc(r_mm.handle, 1)

            def turn_logits(g):
                r_copied.wait(pe, g)
                pass_waits(pe)
                for t in range(T):
                    ins = nc.tensor.transpose(ps[:, 6, 4 * t:4 * t + 4], logits[:, P * t:P * (t + 1)], ident[0:4, 0:4])
                ins.then_inc(r_turned.handle, 1)

            def gate_up(g, j):
                hf, ec = j // EC, j % EC
                if j == 0:
                    x2_split.wait(pe, g, 3)
                if j == EC:
                    x2_split.wait(pe, g)
                if j >= 3:
                    hid_done.wait(pe, g, j - 2)
                for k in range(2):
                    c = C_GU + 2 * P * ec + P * k
                    split_mm(ps[:, GU_BANKS[j % 3][k], 0:HALF], slice(c, c + P),
                             lambda x: x2t[:, x, HALF * hf:HALF * (hf + 1)], False).then_inc(gu_done.handle, 1)

            def down(n, u, tail=False):
                t, e, bank = unit(u, tail)
                if u == 0:
                    hid_done.wait(pe, n, EC + EC // 2)
                if u == FIRST:
                    hid_done.wait(pe, n)
                if u >= 2:
                    comb_done.wait(pe, n, u if u > FIRST and u != WITH_VALUES - 1 and not tail else u - 1)
                for c in range(CH):
                    ins = mm(ps[:, bank, 0:D], hid[:, CH * e + c, P * t:P * (t + 1)], w_down[:, CH * e + c],
                             start=(c == 0), stop=(c == CH - 1))
                ins.then_inc(down_done.handle, 1)

            pe.wait_ge(tab_loaded, 32)
            for i in range(2):
                n = NORD * S // 2
                ins = mm(ps[0:HEADS, 6 + i, 0:n], alpha_t, cheb[:, n * i:n * (i + 1)], start=True, stop=True)
            ins.then_inc(tab_mm, 1)
            pe.wait_ge(small_loaded, 16 * 5)
            conv(0)
            pe.wait_ge(tab_ready, 1)
            for t in range(T):
                turn_x1(0, t)
            x1_split.wait(pe, 0)
            pe.wait_ge(w_split, 1)
            for i in range(2 * QKC):
                qk(0, i)
            pe.wait_ge(tables_in, 16 * 4)
            pe.wait_ge(k_tail_in, 16)

            def group(g, first=False, left=1):
                if not first:
                    r_z.wait(pe, g - 1)
                    qk_sub.wait(pe, g)
                    down(g - 1, 0)
                    hid_done.wait(pe, g - 1)
                stacks_in.wait(pe, g)
                for s in range(NB * QUADS):
                    scores_by_query(g, s)
                    if not first and s < FIRST - 1:
                        down(g - 1, s + 1)
                    if first and s == 10:
                        pe.wait_ge(w_split, 2)
                    if not first and s == 10:
                        comb_done.wait(pe, g - 1, FIRST)
                    if s == 10:
                        values_all(g)
                values(g, 0)
                values(g, 1)
                max_done.wait(pe, g)
                nc.tensor.transpose(ps[:, 5, 0:P], mx[:], ident[:]).then_inc(mt_done.handle, 1)
                if first:
                    pe.wait_ge(late_loaded, 16 * 3)
                pick_img_values(g)
                for i in range(4):
                    if i < 2:
                        values(g, i + 2)
                    if left and i == 2:
                        v_txt_done.wait(pe, g, 2)
                        conv(g + 1)
                    if i == 3:
                        v_img_done.wait(pe, g)
                    if not first:
                        down(g - 1, FIRST + i)
                if left:
                    img_tokens.wait(pe, g + 1)
                v_txt_done.wait(pe, g)

                def event(what, i):
                    if what == "ctx":
                        turn_ctx(g, i)
                    if what == "x2":
                        turn_x2(g, i, first, left)
                    if what == "router":
                        router(g, left)
                    if what == "logits":
                        turn_logits(g)
                    if what == "unit" and not first:
                        pv_copied.wait(pe, g, NB * QUADS - (i < E * T - 1))
                        down(g - 1, i)
                    if left:
                        if what == "x1":
                            if i < 2:
                                added.wait(pe, g, i + 4)
                            turn_x1(g + 1, i)
                        if what == "qk":
                            if i == 0:
                                x1_split.wait(pe, g + 1)
                            if i < 2:
                                x2_split.wait(pe, g, i + 4)
                            qk(g + 1, i)

                for s in range(NB * QUADS + 1):
                    if s < NB * QUADS:
                        scores_by_key(g, s)
                        if not first:
                            for u in unit_after(s):
                                if s > 7:
                                    x2_split.wait(pe, g, 1)
                                down(g - 1, u)
                    if s == 2 and not first:
                        comb_done.wait(pe, g - 1, WITH_VALUES)
                    if s:
                        context(g, s - 1)
                    for what, i in among(s):
                        event(what, i)
                if first:
                    pe.wait_ge(w_split, 8)
                    pe.wait_ge(down_loaded, 16)
                for j in range(2 * EC):
                    if j == 2 and not first:
                        comb_done.wait(pe, g - 1)
                    gate_up(g, j)
                    for what, i in between(j):
                        event(what, i)

            group(0, first=True)
            with pe.Fori(1, G - 1) as g:
                group(g)
            group(G - 1, left=0)
            for u in range(E * T):
                down(G - 1, u, tail=True)


def chebyshev_tables():
    import numpy as np

    def orders(x):
        t = [np.ones_like(x), x]
        while len(t) < NORD:
            t.append(2 * x * t[-1] - t[-2])
        return np.stack(t)

    c = (S - 1) / 2
    order = np.concatenate([np.arange(IMG, S), np.arange(IMG)])
    u = (order - c) / c
    nodes = np.cos(np.pi * (np.arange(NORD) + 0.5) / NORD)
    cheb = np.linalg.inv(orders(nodes).T) @ orders((nodes[:, None] - u[None, :]) / 2)
    cheb[:, 1] /= c
    keys = orders(u)
    keys[1] *= c
    return 4 * cheb, keys


def kernel(**inputs):
    import ml_dtypes
    import numpy as np
    import concourse.bacc as bacc
    from concourse.bass_utils import run_bass_kernel_spmd as run

    i = {k: np.asarray(x) for k, x in inputs.items()}
    f32, bf16 = np.float32, ml_dtypes.bfloat16
    side, patch = 5, 16
    x = i["x"][:, :, :side * patch, :side * patch].reshape(G, NB, 3, side, patch, side, patch)
    x = x.transpose(0, 2, 4, 6, 1, 3, 5).reshape(G, KCONV, P, NB, IMG)
    patches = np.zeros((G, P, KCONV, NB, 32), f32)
    patches[..., :IMG] = x.transpose(0, 2, 1, 3, 4)
    w_conv = i["L0_tok_conv_w"].reshape(D, KCONV, P).transpose(2, 1, 0)
    grid = np.searchsorted(np.arange(1, 32, dtype=f32) / f32(32), np.arange(side, dtype=f32) * f32(0.2), side="right")
    ids = (grid[:, None] * 32 + grid[None, :]).reshape(-1)
    pos = np.zeros((NB, 32, D), f32)
    pos[:, :IMG] = i["L0_tok_pos_table"][ids]
    conv_b = np.zeros((NB, 32, D), f32)
    conv_b[:, :IMG] = i["L0_tok_conv_b"]

    gate = [i["L0_ffn_shared_gate"]] + list(i["L0_ffn_routed_gate"])
    up = [i["L0_ffn_shared_up"]] + list(i["L0_ffn_routed_up"])
    downs = [i["L0_ffn_shared_down"]] + list(i["L0_ffn_routed_down"])
    w = np.zeros((D, WCOLS), f32)
    by_dim = np.arange(D).reshape(HEADS, HD).T.reshape(-1)
    for n, name in enumerate(("Wq", "Wk", "Wv")):
        w[:, D * n:D * (n + 1)] = i["L0_attn_" + name].T[:, by_dim if n < 2 else slice(None)]
    w[:, C_R:C_R + 3] = i["L0_ffn_router_w"]
    for e in range(E):
        for c in range(CH):
            at = C_GU + 2 * P * (CH * e + c)
            w[:, at:at + P] = gate[e][:, P * c:P * (c + 1)]
            w[:, at + P:at + 2 * P] = up[e][:, P * c:P * (c + 1)]
    w = np.stack([w[:P], np.concatenate([w[P:], w[P:]])], 1)
    w = w.reshape(P, 2, 8, WPIECE).transpose(2, 0, 1, 3)
    w_down = np.stack([d[P * c:P * (c + 1)] for d in downs for c in range(CH)], 1)
    bqk = np.concatenate([i["L0_attn_bq"][by_dim], i["L0_attn_bk"][by_dim]]).reshape(QKC, P).T

    cheb, keys = chebyshev_tables()
    k_tail = np.zeros((P - BIAS0, HEADS, NB, PAD), bf16)
    kh = keys.astype(f32).astype(bf16)
    rest = keys.astype(f32) - kh.astype(f32)
    km = rest.astype(bf16)
    kl = (rest - km.astype(f32)).astype(bf16)
    rows = [kh, kh, kh, km[2:], km[2:], kl[2:], np.ones((2, S), bf16)]
    k_tail[..., :S] = np.concatenate(rows)[:, None, None, :]

    pick = np.zeros((NB, 32, NB, 32), f32)
    for b in range(NB):
        pick[b, :IMG, b, :IMG] = np.eye(IMG, dtype=f32)

    arrays = {
        "ids": i["x_txt"].reshape(G, NB, TXT).transpose(0, 2, 1),
        "patches": patches.reshape(G, P, KCONV, P),
        "table": i["L0_txt_weight"],
        "w_conv": w_conv,
        "pos": pos.reshape(P, D),
        "conv_b": conv_b.reshape(P, D),
        "bv": np.broadcast_to(i["L0_attn_bv"], (P, D)),
        "bqk": bqk,
        "r_bias": np.broadcast_to(i["L0_ffn_routing_bias"], (P, T, 3)),
        "w_split": w,
        "w_down": w_down,
        "ident": np.eye(P, dtype=f32),
        "pick": pick.reshape(P, NB, 32),
        "alpha_t": i["L0_attn_alphas"].T,
        "cheb": cheb.reshape(NORD, NORD * S).astype(f32),
        "k_tail": k_tail.reshape(P - BIAS0, HEADS * COLS),
    }
    arrays = {k: np.ascontiguousarray(x) for k, x in arrays.items()}
    nc = bacc.Bacc("TRN2", target_bir_lowering=False, num_devices=1)
    aps = {k: nc.dram_tensor("in_" + k, x.shape, mybir.dt.from_np(x.dtype), kind="ExternalInput").ap() for k, x in arrays.items()}
    aps["out"] = nc.dram_tensor("out", (B, S, D), F32, kind="ExternalOutput").ap()
    build(nc, aps)
    r = run(nc, [{"in_" + k: x for k, x in arrays.items()}], core_ids=[0])
    return r.results[0]["out"]
```
